# Optimizing a Trainium2 kernel written in Bass

```python
import numpy as np
import jax
import jax.numpy as jnp

def _softmax(x, axis=-1):
    return jax.nn.softmax(x, axis=axis)

def _gelu(x):
    return jax.nn.gelu(x, approximate=True)

def _silu(x):
    return jax.nn.silu(x)

def _sigmoid(x):
    return jax.nn.sigmoid(x)

def _layernorm(x, axis=-1, eps=1e-05):
    m = jnp.mean(x, axis=axis, keepdims=True)
    v = jnp.var(x, axis=axis, keepdims=True)
    return (x - m) / jnp.sqrt(v + eps)

def _scatter_add(tgt, idx, src, axis=0):
    return tgt.at[idx].add(src)

def _segment_sum(src, seg, n):
    return jax.ops.segment_sum(src, seg, n)
kernel_name = 'mk_seq_preln_d1_jaxref_r8_c625b3'

def setup_inputs(seed: int=0):
    np.random.seed(seed)
    _w = jnp.asarray

    def _L0_attn_setup():
        import jax, jax.numpy as jnp
        import numpy as np
        EMBED = 256
        HEADS = 16
        NOPE = 128
        VDIM = 128
        ROPE = 64
        Q_HEAD = NOPE + ROPE
        KV_RANK = 64
        BASE = 10000.0

        def _rope(x, offset=0):
            d = x.shape[-1]
            n = x.shape[-2]
            theta = BASE ** (-2.0 * jnp.arange(d // 2, dtype=jnp.float32) / d)
            pos = jnp.arange(n, dtype=jnp.float32) + offset
            ang = pos[:, None] * theta[None, :]
            cos, sin = (jnp.cos(ang), jnp.sin(ang))
            x1 = x[..., 0::2]
            x2 = x[..., 1::2]
            o1 = x1 * cos - x2 * sin
            o2 = x1 * sin + x2 * cos
            return jnp.stack([o1, o2], axis=-1).reshape(x.shape)
        key = jax.random.key(seed)
        ks = jax.random.split(key, 6)
        b, n = (2, 256)
        s = lambda fin: 1.0 / np.sqrt(fin)
        return {'x': jax.random.normal(ks[0], (b, n, EMBED), jnp.float32), 'Wqa': jax.random.normal(ks[1], (EMBED, 64), jnp.float32) * s(EMBED), 'Wqb': jax.random.normal(ks[2], (64, HEADS * Q_HEAD), jnp.float32) * s(64), 'Wkva': jax.random.normal(ks[3], (EMBED, KV_RANK + ROPE), jnp.float32) * s(EMBED), 'Wkvb': jax.random.normal(ks[4], (KV_RANK, HEADS * (NOPE + VDIM)), jnp.float32) * s(KV_RANK), 'Wout': jax.random.normal(ks[5], (HEADS * VDIM, EMBED), jnp.float32) * s(HEADS * VDIM)}
    _L0_attn_in = _L0_attn_setup()

    def _L0_ffn_setup():
        import jax, jax.numpy as jnp
        import numpy as np
        TOP_K = 8
        NEG_INF = -1000000000.0
        key = jax.random.key(seed)
        ks = jax.random.split(key, 6)
        B, S, H, I, E, G, GS = (1, 256, 256, 176, 64, 8, 8)
        sc = 0.02
        return {'hidden_states': jax.random.normal(ks[0], (B, S, H), jnp.float32), 'gate_w': jax.random.normal(ks[1], (E, H), jnp.float32) * sc, 'mask_up_w': jax.random.normal(ks[2], (G, H, GS), jnp.float32) * sc, 'gate_proj_w': jax.random.normal(ks[3], (G, I, H), jnp.float32) * sc, 'up_proj_w': jax.random.normal(ks[4], (G, I, H), jnp.float32) * sc, 'down_proj_w': jax.random.normal(ks[5], (G, H, I), jnp.float32) * sc, 'inv_map': jnp.arange(G * GS, dtype=jnp.int64).reshape(G, GS)}
    _L0_ffn_in = _L0_ffn_setup()
    _d = {'L0_attn_x': _L0_attn_in['x'], 'L0_attn_Wqa': _L0_attn_in['Wqa'], 'L0_attn_Wqb': _L0_attn_in['Wqb'], 'L0_attn_Wkva': _L0_attn_in['Wkva'], 'L0_attn_Wkvb': _L0_attn_in['Wkvb'], 'L0_attn_Wout': _L0_attn_in['Wout'], 'L0_ffn_gate_w': _L0_ffn_in['gate_w'], 'L0_ffn_mask_up_w': _L0_ffn_in['mask_up_w'], 'L0_ffn_gate_proj_w': _L0_ffn_in['gate_proj_w'], 'L0_ffn_up_proj_w': _L0_ffn_in['up_proj_w'], 'L0_ffn_down_proj_w': _L0_ffn_in['down_proj_w'], 'L0_ffn_inv_map': _L0_ffn_in['inv_map']}
    _x0 = _d['L0_attn_x']
    _d['L0_attn_x'] = jax.random.normal(jax.random.fold_in(jax.random.key(seed), 1), (4, 1024, 256), dtype=_x0.dtype)
    del _x0
    return _d

def reference(L0_attn_x, L0_attn_Wqa, L0_attn_Wqb, L0_attn_Wkva, L0_attn_Wkvb, L0_attn_Wout, L0_ffn_gate_w, L0_ffn_mask_up_w, L0_ffn_gate_proj_w, L0_ffn_up_proj_w, L0_ffn_down_proj_w, L0_ffn_inv_map):

    def _L0_attn_ref(x, Wqa, Wqb, Wkva, Wkvb, Wout):
        import jax, jax.numpy as jnp
        import numpy as np
        EMBED = 256
        HEADS = 16
        NOPE = 128
        VDIM = 128
        ROPE = 64
        Q_HEAD = NOPE + ROPE
        KV_RANK = 64
        BASE = 10000.0

        def _rope(x, offset=0):
            d = x.shape[-1]
            n = x.shape[-2]
            theta = BASE ** (-2.0 * jnp.arange(d // 2, dtype=jnp.float32) / d)
            pos = jnp.arange(n, dtype=jnp.float32) + offset
            ang = pos[:, None] * theta[None, :]
            cos, sin = (jnp.cos(ang), jnp.sin(ang))
            x1 = x[..., 0::2]
            x2 = x[..., 1::2]
            o1 = x1 * cos - x2 * sin
            o2 = x1 * sin + x2 * cos
            return jnp.stack([o1, o2], axis=-1).reshape(x.shape)
        b, n, _ = x.shape
        q = x @ Wqa @ Wqb
        q = q.reshape(b, n, HEADS, Q_HEAD).transpose(0, 2, 1, 3)
        q_nope, q_pe = (q[..., :NOPE], q[..., NOPE:])
        ckv = x @ Wkva
        compressed, k_pe = (ckv[..., :KV_RANK], ckv[..., KV_RANK:])
        k_pe = jnp.broadcast_to(k_pe[:, None], (b, HEADS, n, ROPE))
        kv = compressed @ Wkvb
        kv = kv.reshape(b, n, HEADS, NOPE + VDIM).transpose(0, 2, 1, 3)
        k_nope, v = (kv[..., :NOPE], kv[..., NOPE:])
        q_pe = _rope(q_pe)
        k_pe = _rope(k_pe)
        qf = jnp.concatenate([q_nope, q_pe], axis=-1)
        kf = jnp.concatenate([k_nope, k_pe], axis=-1)
        scale = 1.0 / np.sqrt(Q_HEAD)
        scores = jnp.einsum('bhnd,bhmd->bhnm', qf, kf) * scale
        causal = jnp.tril(jnp.ones((n, n), dtype=bool))
        scores = jnp.where(causal, scores, jnp.finfo(scores.dtype).min)
        attn = jax.nn.softmax(scores, axis=-1)
        out = jnp.einsum('bhnm,bhmd->bhnd', attn, v)
        out = out.transpose(0, 2, 1, 3).reshape(b, n, HEADS * VDIM)
        return out @ Wout

    def _L0_ffn_ref(hidden_states, gate_w, mask_up_w, gate_proj_w, up_proj_w, down_proj_w, inv_map):
        import jax, jax.numpy as jnp
        import numpy as np
        TOP_K = 8
        NEG_INF = -1000000000.0
        B, S, H = hidden_states.shape
        x = hidden_states.reshape(-1, H)
        N = x.shape[0]
        E = gate_w.shape[0]
        scores = jax.nn.softmax(x @ gate_w.T, axis=-1)
        topk_w, topk_idx = jax.lax.top_k(scores, TOP_K)
        w_e = jnp.zeros((N, E), x.dtype).at[jnp.arange(N)[:, None], topk_idx].add(topk_w)
        flat = w_e[:, inv_map]
        scalar = flat.sum(-1)
        soft = jax.nn.softmax(jnp.where(flat == 0, NEG_INF, flat), axis=-1)
        xg = x[:, None, :] + jnp.einsum('ngi,ghi->ngh', soft, mask_up_w)
        g = jnp.einsum('ngh,gih->ngi', xg, gate_proj_w)
        u = jnp.einsum('ngh,gih->ngi', xg, up_proj_w)
        a = jax.nn.silu(g) * u
        d = jnp.einsum('ngi,ghi->ngh', a, down_proj_w)
        y = jnp.einsum('ng,ngh->nh', scalar, d)
        return y.reshape(B, S, H)
    x = L0_attn_x
    x = x + _L0_attn_ref(_layernorm(x, axis=-1), L0_attn_Wqa, L0_attn_Wqb, L0_attn_Wkva, L0_attn_Wkvb, L0_attn_Wout)
    x = x + _L0_ffn_ref(_layernorm(x, axis=-1), L0_ffn_gate_w, L0_ffn_mask_up_w, L0_ffn_gate_proj_w, L0_ffn_up_proj_w, L0_ffn_down_proj_w, L0_ffn_inv_map)
    return x

_drawn_inputs = setup_inputs


def setup_inputs(seed=0):
    import zlib

    import numpy as np

    out = dict(_drawn_inputs(seed))
    spreads = {}
    factors = {'L0_ffn_gate_w': 8.0,
     'L0_ffn_mask_up_w': 8.0,
     'L0_ffn_gate_proj_w': 8.0,
     'L0_ffn_up_proj_w': 8.0,
     'L0_ffn_down_proj_w': 8.0}
    for name, (base, spread) in spreads.items():
        noise = np.random.default_rng([zlib.crc32(name.encode()), seed]).standard_normal(out[name].shape)
        drawn = base * np.exp(spread * noise) if base else spread * noise
        out[name] = jnp.asarray(drawn.astype(out[name].dtype))
    for name, factor in factors.items():
        out[name] = (out[name] * factor).astype(out[name].dtype)
    return out
```

```python
import numpy as np
import concourse.bass as bass
from concourse import mybir
from contextlib import ExitStack

F32 = mybir.dt.float32
F32R = mybir.dt.float32r
BF16 = mybir.dt.bfloat16
I32 = mybir.dt.int32
ALU = mybir.AluOpType
ACT = mybir.ActivationFunctionType
AX = mybir.AxisListType

B, N, D = 4, 1024, 256
H, NOPE, VD, ROPE = 16, 128, 128, 64
QH = NOPE + ROPE
RANK = 64
P = 128
KC = D // P
NT = N // P
PAIRS = H // 2
SCALE = 1.0 / np.sqrt(QH)
EPS = 1e-5
NEG = -3.0e38
G, GS, I, E, TOPK = 8, 8, 176, 64, 8
GI = G * I
MC = GI // P
GU = 2 * I
QC = 512
NC2 = N // QC
PW = [[(4 * c + j + 1) * P for j in range(4)] for c in range(NC2)]
POFF = [[sum(PW[c][:j]) for j in range(4)] for c in range(NC2)]
PBUF = sum(PW[1])

UNITS = [(0, 0), (1, 0), (0, 1), (1, 1)]
S_BATCH = 4 + 16 * PAIRS
Q_BATCH = 4 + 4 * PAIRS
TU = [4, 4, 8, 8]
T_PAIR = sum(TU)


def mm(nc, out, lhsT, rhs, start, stop):
    return nc.tensor.matmul(out, lhsT, rhs, start=start, stop=stop, skip_group_check=True)


class Spots:

    def __init__(self, tensor):
        self.tensor, self.n = tensor, 0

    def next(self):
        self.n += 1
        return self.tensor[:, self.n:self.n + 1]


def vector_waits(nc, spots, semaphore, value):
    nc.vector.wait_ge(semaphore, value)
    nc.vector.memset(spots.next(), 0.0)


def attention_weights(nc, t, ins):
    with ExitStack() as ctx:
        def sb(name, shape, dt=F32):
            return ctx.enter_context(nc.sbuf_tensor(name, shape, dt))

        def sem(name):
            return ctx.enter_context(nc.semaphore(name))

        wqb = sb("wqb", [P, H * QH])
        wkvb = sb("wkvb", [P, H * (NOPE + VD)])
        wout = sb("wout", [P, H, D])
        wqa = sb("wqa_raw", [P, KC, RANK])
        wkva = sb("wkva_raw", [P, KC, RANK + ROPE])
        mask = sb("mask", [P, P])
        wT = sb("wT", [P, H, 3 * P])
        wq = sb("wq_all", [P, PAIRS, 2, 2, 192], F32R)
        ps = ctx.enter_context(nc.psum_tensor("wps", [P, 8, 512], F32))

        loaded = sem("w_loaded")
        heads_T = sem("heads_transposed")
        heads_T_sb = sem("heads_transposed_in_sbuf")
        prod = sem("head_products")
        prod_h = sem("head_products_high")
        prod_done = sem("head_products_done")
        plain_h = sem("plain_high")
        plain_done = sem("plain_done")
        stored = sem("wq_stored")

        block = ctx.enter_context(nc.Block())
        raw_pe = wqb[:].rearrange("p (r a c) -> p r a c", r=PAIRS, a=2)[:, :, :, NOPE:QH]\
                       .rearrange("p r a (j e) -> p r a j e", e=2)
        raw_kpe = wkva[:, :, RANK:].rearrange("p k (j e) -> p k j e", e=2)

        @block.sync
        def _(sp):
            for r in (0, 64):
                sp.dma_start(wqb[r:r + 64, :], ins["Wqb"]).then_inc(loaded, 16)
                sp.dma_start(wkvb[r:r + 64, :], ins["Wkvb"]).then_inc(loaded, 16)
            sp.dma_start(wqa[:], ins["Wqa"].rearrange("(k p) n -> p k n", p=P)).then_inc(loaded, 16)
            sp.dma_start(wkva[:], ins["Wkva"].rearrange("(k p) n -> p k n", p=P)).then_inc(loaded, 16)
            sp.dma_start(wout[:], ins["Wout"].rearrange("(h p) n -> p h n", p=P)).then_inc(loaded, 16)
            sp.dma_start(t.ident[:], ins["ident"]).then_inc(loaded, 16)
            sp.dma_start(mask[:], ins["mask"]).then_inc(loaded, 16)
            sp.dma_start(t.cosT[:], ins["cos"]).then_inc(loaded, 16)
            sp.dma_start(t.sinT[:], ins["sin"]).then_inc(loaded, 16)
            sp.wait_ge(plain_done, 1)
            sp.wait_ge(prod_done, H)
            for r in range(PAIRS + 1):
                sp.dma_start(t.wq_dram[r], wq[:, r % PAIRS].bitcast(F32)).then_inc(stored, 16)
            sp.wait_ge(stored, 16 * (PAIRS + 1))

        LOADS = 11

        @block.tensor
        def _(pe):
            pe.wait_ge(loaded, 16 * LOADS)
            for h in range(H):
                if h >= 8:
                    pe.wait_ge(heads_T_sb, h - 7)
                srcs = [wqb[:, h * QH:h * QH + NOPE], wkvb[:, h * 256:h * 256 + NOPE],
                        wkvb[:, h * 256 + NOPE:(h + 1) * 256]]
                for k, src in enumerate(srcs):
                    last = nc.tensor.transpose(ps[:, h % 8, k * P:(k + 1) * P], src, t.ident[:])
                last.then_inc(heads_T, 1)
            for h in range(H):
                pe.wait_ge(heads_T_sb, min(h + 9, H))
                if h >= 8:
                    pe.wait_ge(prod_done, h - 7)
                mm(nc, ps[:, h % 8, 0:RANK], wT[:, h, 0:P], wT[:, h, P:P + RANK], True, True)
                mm(nc, ps[:, h % 8, RANK:RANK + D], wT[:, h, 2 * P:3 * P], wout[:, h, :], True, True)\
                    .then_inc(prod, 1)

        @block.scalar
        def _(act):
            act.wait_ge(loaded, 16 * LOADS)
            for k in (0, 1):
                c = slice(32 * k, 32 * k + 32)
                cy = slice(P + 32 * k, P + 32 * k + 32)
                for a in range(2):
                    nc.scalar.mul(wq[:, :, 0, a, c], raw_pe[:, :, a, :, k], SCALE)
                    nc.scalar.mul(wq[:, :, 0, a, cy], raw_pe[:, :, a, :, 1 - k], SCALE)
                nc.scalar.copy(t.wk[:, 0, :, c], raw_kpe[:, :, :, k])
                nc.scalar.copy(t.wk[:, 0, :, cy], raw_kpe[:, :, :, 1 - k])
                nc.scalar.copy(t.wqa[:, 0, :, 64 * k:64 * k + 64], wqa[:])
            nc.scalar.copy(t.wk[:, 0, :, 64:128], wkva[:, :, 0:RANK]).then_inc(plain_h, 1)
            for h in range(H):
                act.wait_ge(heads_T, h + 1)
                nc.scalar.copy(wT[:, h, :], ps[:, h % 8, 0:3 * P]).then_inc(heads_T_sb, 1)
            for h in range(H):
                r = 64 * (h % 2)
                act.wait_ge(prod, h + 1)
                nc.scalar.mul(wq[:, h // 2, 0, h % 2, 64:128], ps[:, h % 8, 0:RANK], SCALE)
                nc.scalar.copy(t.w2h[r:r + 64, h // 2, :], ps[r:r + 64, h % 8, RANK:RANK + D]).then_inc(prod_h, 1)

        @block.vector
        def _(dve):
            dve.wait_ge(loaded, 16 * LOADS)
            nc.vector.tensor_copy(t.ident_b[:], t.ident[:])
            nc.vector.tensor_copy(t.mask_b[:], mask[:])
            dve.wait_ge(plain_h, 1)
            for k in (0, 1):
                c = slice(32 * k, 32 * k + 32)
                cy = slice(P + 32 * k, P + 32 * k + 32)
                for a in range(2):
                    for cols, e in ((c, k), (cy, 1 - k)):
                        nc.vector.scalar_tensor_tensor(out=wq[:, :, 1, a, cols], in0=raw_pe[:, :, a, :, e],
                                                       scalar=float(SCALE), in1=wq[:, :, 0, a, cols].bitcast(F32),
                                                       op0=ALU.mult, op1=ALU.subtract)
                for cols, e in ((c, k), (cy, 1 - k)):
                    nc.vector.tensor_tensor(t.wk[:, 1, :, cols], raw_kpe[:, :, :, e],
                                            t.wk[:, 0, :, cols].bitcast(F32), ALU.subtract)
                nc.vector.tensor_tensor(t.wqa[:, 1, :, 64 * k:64 * k + 64], wqa[:],
                                        t.wqa[:, 0, :, 64 * k:64 * k + 64].bitcast(F32), ALU.subtract)
            nc.vector.tensor_tensor(t.wk[:, 1, :, 64:128], wkva[:, :, 0:RANK],
                                    t.wk[:, 0, :, 64:128].bitcast(F32), ALU.subtract).then_inc(plain_done, 1)
            for h in range(H):
                r = 64 * (h % 2)
                dve.wait_ge(prod_h, h + 1)
                cols = wq[:, h // 2, 0, h % 2, 64:128]
                nc.vector.scalar_tensor_tensor(out=wq[:, h // 2, 1, h % 2, 64:128], in0=ps[:, h % 8, 0:RANK],
                                               scalar=float(SCALE), in1=cols.bitcast(F32),
                                               op0=ALU.mult, op1=ALU.subtract)
                nc.vector.tensor_tensor(t.w2l[r:r + 64, h // 2, :], ps[r:r + 64, h % 8, RANK:RANK + D],
                                        t.w2h[r:r + 64, h // 2, :].bitcast(F32), ALU.subtract).then_inc(prod_done, 1)


def attention(nc, t, ins):
    with ExitStack() as ctx:
        def sb(name, shape, dt=F32):
            return ctx.enter_context(nc.sbuf_tensor(name, shape, dt))

        def sem(name):
            return ctx.enter_context(nc.semaphore(name))

        xb = sb("xb", [P, NT, D])
        kTh, kTl = sb("kTh", [P, N], F32R), sb("kTl", [P, N], F32R)
        vh, vl = sb("vh", [P, NT, 192], F32R), sb("vl", [P, NT, 192], F32R)
        xq = sb("xq", [P, N], F32R)
        wqs = sb("wqs", [P, 2, 2, 192], F32R)
        qh, ql = sb("qh", [P, 2, N], F32R), sb("ql", [P, 2, N], F32R)
        psb = sb("psb", [P, 2, PBUF])
        pTh, pTl = sb("pTh", [P, 3, QC], F32R), sb("pTl", [P, 3, QC], F32R)
        osb = sb("osb", [P, PAIRS, N])
        rot1, rot2 = sb("rot1", [P, 2, QC]), sb("rot2", [64, 2, QC])
        nmax, lsum, linv = sb("nmax", [P, 2, 4]), sb("lsum", [P, 2, 4]), sb("linv", [P, 2, 4])
        lrep, ones = sb("lrep", [P, 4, P]), sb("ones", [P, 4])
        linv_b = sb("linv_b", [P, 2, QC])
        stats, aggr = sb("stats", [P, NT, 6]), sb("aggr", [P, NT, 2])
        vareps, std, rstd = sb("vareps", [P, NT]), sb("std", [P, NT]), sb("rstd", [P, NT])
        spot_v = Spots(sb("spot_v", [1, 64]))
        xn = psb[:, 0, 0:NT * D].rearrange("p (t d) -> p t d", t=NT)

        banks = ctx.enter_context(nc.psum_tensor("aps", [P, 8, 512], F32))
        sps = banks[:, 0:4, :].rearrange("p (s b) n -> p s b n", s=2)
        tps = banks[:, 4:7, :]
        ops = banks[:, 7, :]

        x_loaded, x_stored = sem("x_loaded"), sem("x_stored")
        zeroed = sem("v_zeroed")
        st1, st2, st3, st4, st5 = (sem("stats_done"), sem("aggr_done"), sem("vareps_done"), sem("std_done"),
                                   sem("rstd_done"))
        xn_ready = sem("xn_ready")
        xT_ps, xT_h, xT_l = sem("xT_ps"), sem("xT_h"), sem("xT_l")
        xq_ps, xq_h, xq_rdy = sem("xq_ps"), sem("xq_h"), sem("xq_ready")
        k_ps, k_rot, k_add, k_high, k_rdy = (sem("k_ps"), sem("k_rotated"), sem("k_added"), sem("k_high"),
                                             sem("k_ready"))
        v_ps, v_h, v_rdy = sem("v_ps"), sem("v_h"), sem("v_ready")
        wq_loaded = sem("wq_loaded")
        q_ps, q_rot, q_add, q_high, q_split = (sem("q_ps"), sem("q_rotated"), sem("q_added"), sem("q_high"),
                                               sem("q_split"))
        s_ready, m_ready, e_done = sem("scores_ready"), sem("max_ready"), sem("exp_done")
        l_inv, l_rep, l_ps, l_sb = (sem("rowsums_inverted"), sem("inverses_repeated"), sem("inverses_ps"),
                                    sem("inverses_sb"))
        t_ready, t_high, t_low, pv_done = sem("pT_ready"), sem("pT_high"), sem("pT_low"), sem("pv_done")
        o_sb = sem("o_in_sbuf")
        oh_rdy, ol_rdy, y_used, y_ready, x2_ready = (sem("o_high"), sem("o_low"), sem("o_projected"),
                                                     sem("y_ready"), sem("x2_ready"))

        block = ctx.enter_context(nc.Block())
        x_v = ins["x"].rearrange("b (t p) d -> b p t d", p=P)
        x2_v = t.x2_dram.rearrange("b (t p) d -> b p t d", p=P)

        def s_(v, j):
            return ("s", v, j)

        PROLOGUE = [("q", q, 0) for q in range(4)] + [s_(0, j) for j in range(4)]
        BODY = [[s_(1, j) for j in range(4)],
                [s_(2, 0), s_(2, 1), s_(2, 2), ("l", 0, 0), s_(2, 3)],
                [s_(3, 0), ("q", 4, 0), s_(3, 1), ("q", 5, 0), s_(3, 2), ("q", 6, 0), s_(3, 3)],
                [s_(4, 0), s_(4, 1), ("q", 7, 0), ("l", 1, 0), s_(4, 2), s_(4, 3)]]
        FLAT = [x for g in BODY for x in g]
        assert len(FLAT) % 2 == 0 and len(PROLOGUE) % 2 == 0 and T_PAIR % 3 == 0
        SLOT = {x: n % 2 for n, x in enumerate(PROLOGUE)}
        BEFORE = {x: PROLOGUE[n - 2] if n >= 2 else None for n, x in enumerate(PROLOGUE)}
        BSLOT = {x: n % 2 for n, x in enumerate(FLAT)}
        BBEFORE = {}
        for n, x in enumerate(FLAT):
            if n >= 2:
                BBEFORE[x] = FLAT[n - 2]
            else:
                k, v, j = FLAT[n - 2]
                BBEFORE[x] = (k, v - 4, j)

        def s_index(v, j):
            return 4 * v + j

        def plan(g):
            first = sum(TU[:g])
            n = TU[g]
            ts = [("t", first + k) for k in range(n)]
            xs = [("x", x) for x in BODY[g]]
            out = xs[:2]
            rest = xs[2:]
            parts = len(rest) + 1
            for k in range(parts):
                out += ts[k * n // parts:(k + 1) * n // parts]
                out += rest[k:k + 1]
            return out

        PLAN = [plan(g) for g in range(4)]

        def t_unit(n):
            u = next(u for u in range(4) if n < sum(TU[:u + 1]))
            return u, n - sum(TU[:u])

        def t_cols(n):
            u, kb = t_unit(n)
            return max(0, kb - 4 * UNITS[u][1]) * P

        @block.sync
        def _(sp):
            with sp.Fori(0, B) as b:
                sp.wait_ge(x_stored, b * 16 + 1)
                sp.dma_start(xb[:], x_v[bass.ds(b, 1)].rearrange("a p t d -> (a p) t d")).then_inc(x_loaded, 16)
                sp.dma_start(wqs[:].bitcast(F32), t.wq_dram[0]).then_inc(wq_loaded, 16)
                with sp.Fori(0, PAIRS) as r:
                    sp.wait_ge(q_ps, b * Q_BATCH + r * 4 + 4)
                    sp.dma_start(wqs[:].bitcast(F32), t.wq_dram[bass.ds(r + 1, 1)].rearrange("a p l h c -> (a p) l h c"))\
                        .then_inc(wq_loaded, 16)
                sp.wait_ge(q_ps, b * Q_BATCH + Q_BATCH)
                sp.wait_ge(x2_ready, b * NT + NT)
                sp.dma_start(x2_v[bass.ds(b, 1)].rearrange("a p t d -> (a p) t d"), xb[:]).then_inc(x_stored, 16)
            sp.wait_ge(x_stored, 16 * B + 1)

        @block.tensor
        def _(pe):
            with pe.Fori(0, B) as b:
                for n in range(4):
                    k, g = n // 2, n % 2
                    pe.wait_ge(xn_ready, b * NT + 4 * (g + 1))
                    for i in range(4):
                        last = nc.tensor.transpose(banks[:, n, i * P:(i + 1) * P],
                                                   xn[:, 4 * g + i, k * P:(k + 1) * P], t.ident[:])
                    last.then_inc(xT_ps, 1)
                pe.wait_ge(xT_l, b * 4 + 4)

                def project(out, w, cols, c):
                    for k in range(KC):
                        for n, (wp, xp) in enumerate(((0, qh), (0, ql), (1, qh))):
                            last = mm(nc, out, w[:, wp, k, cols], xp[:, k, c * QC:(c + 1) * QC],
                                      k == 0 and n == 0, k == KC - 1 and n == 2)
                    return last

                for c in range(NC2):
                    project(banks[:, 4 + c, :], t.wqa, slice(0, P), c).then_inc(xq_ps, 1)
                for c in range(NC2):
                    kb = (6, 0)[c]
                    project(banks[:, kb, :], t.wk, slice(0, P), c)
                    project(banks[0:64, kb + 1, :], t.wk, slice(P, 192), c).then_inc(k_ps, 1)
                for g in range(2):
                    for i in range(4):
                        tok = slice((4 * g + i) * P, (4 * g + i + 1) * P)
                        out = banks[:, 2 + g, i * 64:(i + 1) * 64]
                        for k in range(KC):
                            for n, (xp, wp) in enumerate(((qh, 0), (qh, 1), (ql, 0))):
                                last = mm(nc, out, xp[:, k, tok], t.wk[:, wp, k, 64:128],
                                          k == 0 and n == 0, k == KC - 1 and n == 2)
                    last.then_inc(v_ps, 1)

                def q_job(slot, q, base):
                    a, c = UNITS[q % 4]
                    if q % 4 == 0:
                        pe.wait_ge(wq_loaded, base)
                    rhs = xq[:, c * QC:(c + 1) * QC]
                    for wp in range(2):
                        mm(nc, sps[:, slot, 0, :], wqs[:, wp, a, 0:P], rhs, wp == 0, wp == 1)
                    for wp in range(2):
                        last = mm(nc, sps[0:64, slot, 1, :], wqs[:, wp, a, P:192], rhs, wp == 0, wp == 1)
                    last.then_inc(q_ps, 1)

                def s_job(slot, v, j, qbase):
                    a, c = UNITS[v % 4]
                    if j == 0:
                        pe.wait_ge(q_split, qbase + v + 1)
                    w = PW[c][j]
                    tok = slice((4 * c + j) * P, (4 * c + j + 1) * P)
                    segs = [(s, min(QC, w - s)) for s in range(0, w, QC)]
                    for n, (q, ks) in enumerate(((qh, (kTh, kTl)), (ql, (kTh,)))):
                        for i, (s, m) in enumerate(segs):
                            for kk, kt in enumerate(ks):
                                diag = s + m == w
                                last = mm(nc, sps[:, slot, i, 0:m], q[:, a, tok], kt[:, s:s + m],
                                          n == 0 and kk == 0, n == 1 and not diag)
                    i = len(segs) - 1
                    m = segs[i][1]
                    mm(nc, sps[:, slot, i, m - P:m], t.ident_b[:], t.mask_b[:], False, True).then_inc(s_ready, 1)

                def slot_free(before, sbase, qbase, obase=None):
                    if before is None:
                        return
                    kind, v, j = before
                    if kind == "s":
                        pe.wait_ge(e_done, sbase + s_index(v, j) + 1)
                    elif kind == "q":
                        pe.wait_ge(q_rot, qbase + v + 1)
                    else:
                        pe.wait_ge(l_sb, obase + v + 1)

                sb0, qb0 = b * S_BATCH, b * Q_BATCH
                pe.wait_ge(xq_rdy, b * 2 + 2)
                pe.wait_ge(k_rdy, b * 2 + 2)
                pe.wait_ge(v_rdy, b * 2 + 2)
                for x in PROLOGUE:
                    slot_free(BEFORE[x], sb0, qb0)
                    if x[0] == "q":
                        q_job(SLOT[x], x[1], b * (16 * (PAIRS + 1)) + 16)
                    else:
                        s_job(SLOT[x], x[1], x[2], qb0)

                with pe.Fori(0, PAIRS) as r:
                    sbase = pe.snap(b * S_BATCH + r * 16)
                    qbase = pe.snap(b * Q_BATCH + r * 4)
                    wbase = pe.snap(b * (16 * (PAIRS + 1)) + r * 16 + 32)
                    tbase = pe.snap(b * (PAIRS * T_PAIR) + r * T_PAIR)
                    obase = pe.snap(b * (PAIRS * 2) + r * 2)

                    def t_job(n):
                        u, kb = t_unit(n)
                        if kb == 0:
                            pe.wait_ge(e_done, sbase + 4 * u + 4)
                        pe.wait_ge(t_low, tbase + n + 1)
                        for j in range(t_cols(n) // P, 4):
                            off = POFF[UNITS[u][1]][j] + kb * P
                            last = nc.tensor.transpose(tps[:, n % 3, j * P:(j + 1) * P],
                                                       psb[:, u % 2, off:off + P], t.ident[:])
                        last.then_inc(t_ready, 1)

                    def pv_job(n):
                        u, kb = t_unit(n)
                        a, c = UNITS[u]
                        if a == 0 and kb == 0:
                            pe.wait_ge(o_sb, obase + c + 1)
                        pe.wait_ge(t_low, tbase + n + 4)
                        s = t_cols(n)
                        cols = slice(64, 192) if a == 0 else slice(0, P)
                        for i, (v, pt) in enumerate(((vh, pTh), (vl, pTh), (vh, pTl))):
                            last = mm(nc, ops[:, s:QC], v[:, kb, cols], pt[:, n % 3, s:QC],
                                      a == 0 and kb == 0 and i == 0, a == 1 and kb == TU[u] - 1 and i == 2)
                        last.then_inc(pv_done, 1)

                    pending = []
                    for g in range(4):
                        for what, x in PLAN[g]:
                            if what == "x":
                                slot_free(BBEFORE[x], sbase, qbase, obase)
                                if x[0] == "q":
                                    q_job(BSLOT[x], x[1], wbase)
                                elif x[0] == "l":
                                    pe.wait_ge(l_rep, 2 * obase + 2 * x[1] + 3)
                                    for j in range(4):
                                        last = nc.tensor.transpose(sps[:, BSLOT[x], 0, j * P:(j + 1) * P],
                                                                   lrep[:, j, :], t.ident[:])
                                    last.then_inc(l_ps, 1)
                                else:
                                    s_job(BSLOT[x], x[1], x[2], qbase)
                            else:
                                t_job(x)
                                pending.append(x)
                                if len(pending) > 2:
                                    pv_job(pending.pop(0))
                    for n in pending:
                        pv_job(n)

                pe.wait_ge(e_done, b * S_BATCH + S_BATCH)
                pe.wait_ge(o_sb, b * (PAIRS * 2) + PAIRS * 2 + 1)
                for pr in range(PAIRS):
                    pe.wait_ge(ol_rdy, b * PAIRS + pr + 1)
                    for i in range(NT):
                        tok = slice(i * P, (i + 1) * P)
                        for n, (o, w) in enumerate(((qh, t.w2h), (qh, t.w2l), (ql, t.w2h))):
                            last = mm(nc, banks[:, i, 0:D], o[:, pr % 2, tok], w[:, pr, :],
                                      pr == 0 and n == 0, pr == PAIRS - 1 and n == 2)
                        if pr == PAIRS - 1:
                            last.then_inc(y_ready, 1)
                    if pr < PAIRS - 1:
                        last.then_inc(y_used, 1)

        @block.scalar
        def _(act):
            with act.Fori(0, B) as b:
                act.wait_ge(st3, b + 1)
                nc.scalar.activation(std[:], vareps[:], ACT.Sqrt).then_inc(st4, 1)
                for n in range(4):
                    k, g = n // 2, n % 2
                    act.wait_ge(xT_ps, b * 4 + n + 1)
                    nc.scalar.copy(qh[:, k, g * QC:(g + 1) * QC], banks[:, n, :]).then_inc(xT_h, 1)
                for c in range(NC2):
                    act.wait_ge(xq_ps, b * 2 + c + 1)
                    nc.scalar.copy(xq[:, c * QC:(c + 1) * QC], banks[:, 4 + c, :]).then_inc(xq_h, 1)
                for g in range(2):
                    act.wait_ge(v_ps, b * 2 + g + 1)
                    if g == 0:
                        act.wait_ge(zeroed, 2)
                    nc.scalar.copy(vh[:, 4 * g:4 * g + 4, 64:128],
                                   banks[:, 2 + g, 0:256].rearrange("p (t c) -> p t c", t=4)).then_inc(v_h, 1)

                for c in range(NC2):
                    cols = slice(c * QC, (c + 1) * QC)
                    act.wait_ge(k_add, b * 2 + c + 1)
                    nc.scalar.copy(kTh[:, cols], rot1[:, c, :]).then_inc(k_high, 1)

                def q_high_job(q, qbase):
                    a, c = UNITS[q % 4]
                    act.wait_ge(q_add, qbase + q + 1)
                    nc.scalar.copy(qh[:, a, c * QC:(c + 1) * QC], rot1[:, q % 2, :]).then_inc(q_high, 1)

                def exp_job(v, j, sbase):
                    c = UNITS[v % 4][1]
                    off, w = POFF[c][j], PW[c][j]
                    act.wait_ge(m_ready, sbase + s_index(v, j) + 1)
                    slot = BSLOT[s_(v, j)] if v else SLOT[s_(v, j)]
                    nc.scalar.activation(psb[:, v % 2, off:off + w],
                                         sps[:, slot, :, :].rearrange("p b n -> p (b n)")[:, 0:w], ACT.Exp,
                                         bias=nmax[:, v % 2, j:j + 1], scale=1.0,
                                         accum_out=lsum[:, v % 2, j:j + 1]).then_inc(e_done, 1)

                sb0 = b * S_BATCH
                for q in range(4):
                    q_high_job(q, b * Q_BATCH)
                for j in range(4):
                    exp_job(0, j, sb0)
                with act.Fori(0, PAIRS) as r:
                    sbase = act.snap(b * S_BATCH + r * 16)
                    qbase = act.snap(b * Q_BATCH + r * 4)
                    tbase = act.snap(b * (PAIRS * T_PAIR) + r * T_PAIR)
                    obase = act.snap(b * (PAIRS * 2) + r * 2)
                    def high_job(n):
                        s = t_cols(n)
                        act.wait_ge(t_ready, tbase + n + 1)
                        act.wait_ge(pv_done, tbase + n + 1)
                        nc.scalar.copy(pTh[:, n % 3, s:QC], tps[:, n % 3, s:QC]).then_inc(t_high, 1)

                    def l_job(c):
                        act.wait_ge(l_ps, obase + c + 2)
                        slot = BSLOT[("l", c, 0)]
                        nc.scalar.copy(linv_b[:, c, :], sps[:, slot, 0, :]).then_inc(l_sb, 1)

                    late = []
                    for g in range(4):
                        due = []
                        for what, x in PLAN[g]:
                            for d in due:
                                d[1] -= 1
                            if due and due[0][1] < 0:
                                q_high_job(due.pop(0)[0], qbase)
                            if what == "x" and x[0] == "q":
                                due.append([x[1], 2])
                            if what == "t":
                                high_job(x)
                            elif x[0] == "l":
                                l_job(x[1])
                            if late and (what == "t" or x[0] == "s"):
                                exp_job(*late.pop(), sbase)
                            if what == "x" and x[0] == "s":
                                late.append(x[1:])
                        for d in due:
                            q_high_job(d[0], qbase)
                    for x in late:
                        exp_job(*x, sbase)
                act.wait_ge(q_split, b * Q_BATCH + Q_BATCH)
                for pr in range(PAIRS):
                    if pr >= 2:
                        act.wait_ge(y_used, b * (PAIRS - 1) + pr - 1)
                    nc.scalar.copy(qh[:, pr % 2, :], osb[:, pr, :]).then_inc(oh_rdy, 1)

        @block.vector
        def _(dve):
            nc.vector.memset(spot_v.tensor[:], 0.0).then_inc(x_stored, 1)
            nc.vector.memset(vh[:].bitcast(F32), 0.0).then_inc(zeroed, 1)
            nc.vector.memset(vl[:].bitcast(F32), 0.0).then_inc(zeroed, 1)
            nc.vector.memset(nmax[:], 0.0).then_inc(t_low, 3)
            nc.vector.memset(lsum[:], 0.0).then_inc(pv_done, 3)
            nc.vector.memset(linv[:], 0.0).then_inc(o_sb, 1)
            nc.vector.memset(linv_b[:], 0.0).then_inc(l_ps, 1)
            with dve.Fori(0, B) as b:
                dve.wait_ge(x_loaded, b * 16 + 16)
                for i in range(NT):
                    nc.vector.bn_stats(stats[:, i, :], xb[:, i, :]).then_inc(st1, 1)
                vector_waits(nc, spot_v, st1, b * NT + NT)
                for i in range(NT):
                    nc.vector.bn_aggr(aggr[:, i, :], stats[:, i, :]).then_inc(st2, 1)
                dve.wait_ge(st2, b * NT + NT)
                nc.vector.tensor_scalar(vareps[:], aggr[:, :, 1], EPS, None, ALU.add).then_inc(st3, 1)
                dve.wait_ge(st4, b + 1)
                nc.vector.reciprocal(rstd[:], std[:]).then_inc(st5, 1)
                dve.wait_ge(st5, b + 1)
                for i in range(NT):
                    nc.vector.tensor_scalar(xn[:, i, :], xb[:, i, :], aggr[:, i, 0:1], rstd[:, i:i + 1],
                                            ALU.subtract, ALU.mult).then_inc(xn_ready, 1)
                for n in range(4):
                    k, g = n // 2, n % 2
                    dve.wait_ge(xT_h, b * 4 + n + 1)
                    cols = slice(g * QC, (g + 1) * QC)
                    nc.vector.tensor_tensor(ql[:, k, cols], banks[:, n, :], qh[:, k, cols].bitcast(F32),
                                            ALU.subtract).then_inc(xT_l, 1)
                for c in range(NC2):
                    cols = slice(c * QC, (c + 1) * QC)
                    dve.wait_ge(xq_h, b * 2 + c + 1)
                    nc.vector.tensor_tensor(xq[64:128, cols], banks[64:128, 4 + c, :], xq[64:128, cols].bitcast(F32),
                                            ALU.subtract).then_inc(xq_rdy, 1)
                for c in range(NC2):
                    cols = slice(c * QC, (c + 1) * QC)
                    kb = (6, 0)[c]
                    dve.wait_ge(k_ps, b * 2 + c + 1)
                    nc.vector.tensor_tensor(rot1[:, c, :], banks[:, kb, :], t.cosT[:, cols], ALU.mult)
                    nc.vector.tensor_tensor(rot2[:, c, :], banks[0:64, kb + 1, :], t.sinT[:, cols],
                                            ALU.mult).then_inc(k_rot, 1)
                for g in range(2):
                    dve.wait_ge(v_h, b * 2 + g + 1)
                    nc.vector.tensor_tensor(vl[:, 4 * g:4 * g + 4, 64:128],
                                            banks[:, 2 + g, 0:256].rearrange("p (t c) -> p t c", t=4),
                                            vh[:, 4 * g:4 * g + 4, 64:128].bitcast(F32), ALU.subtract).then_inc(v_rdy, 1)

                def max_job(v, j, sbase):
                    c = UNITS[v % 4][1]
                    dve.wait_ge(s_ready, sbase + s_index(v, j) + 1)
                    slot = BSLOT[s_(v, j)] if v else SLOT[s_(v, j)]
                    nc.vector.tensor_reduce(out=nmax[:, v % 2, j:j + 1],
                                            in_=sps[:, slot, :, :].rearrange("p b n -> p (b n)")[:, 0:PW[c][j]],
                                            axis=AX.X, op=ALU.max, negate=True).then_inc(m_ready, 1)

                def inv_job(v, sbase, rep=None):
                    dve.wait_ge(e_done, sbase + s_index(v, 3) + 1)
                    if rep is not None:
                        dve.wait_ge(l_rep, rep)
                    nc.vector.reciprocal(linv[:, v % 2, :], lsum[:, v % 2, :]).then_inc(l_inv, 1)

                def rot_job(slot, q, qbase):
                    c = UNITS[q % 4][1]
                    cols = slice(c * QC, (c + 1) * QC)
                    dve.wait_ge(q_ps, qbase + q + 1)
                    if q >= 2:
                        dve.wait_ge(q_split, qbase + q - 1)
                    nc.vector.tensor_tensor(rot1[:, q % 2, :], sps[:, slot, 0, :], t.cosT[:, cols], ALU.mult)
                    nc.vector.tensor_tensor(rot2[:, q % 2, :], sps[0:64, slot, 1, :], t.sinT[:, cols],
                                            ALU.mult).then_inc(q_rot, 1)

                dve.wait_ge(k_rdy, b * 2 + 2)
                sb0, qb0 = b * S_BATCH, b * Q_BATCH
                for x in PROLOGUE:
                    if x[0] == "q":
                        rot_job(SLOT[x], x[1], qb0)
                    else:
                        max_job(x[1], x[2], sb0)
                inv_job(0, sb0)
                with dve.Fori(0, PAIRS) as r:
                    sbase = dve.snap(b * S_BATCH + r * 16)
                    qbase = dve.snap(b * Q_BATCH + r * 4)
                    tbase = dve.snap(b * (PAIRS * T_PAIR) + r * T_PAIR)
                    obase = dve.snap(b * (PAIRS * 2) + r * 2)
                    rbase = dve.snap(b * (PAIRS * 4) + r * 4)

                    def low_job(n):
                        s = t_cols(n)
                        dve.wait_ge(t_high, tbase + n + 1)
                        nc.vector.tensor_tensor(pTl[:, n % 3, s:QC], tps[:, n % 3, s:QC],
                                                pTh[:, n % 3, s:QC].bitcast(F32), ALU.subtract).then_inc(t_low, 1)

                    def o_job(c):
                        dve.wait_ge(pv_done, tbase + sum(TU[:2 * c + 2]) + 3)
                        dve.wait_ge(l_sb, obase + c + 1)
                        nc.vector.tensor_tensor(osb[:, bass.ds(r, 1), c * QC:(c + 1) * QC]
                                                .rearrange("p a n -> p (a n)"),
                                                ops, linv_b[:, c, :], ALU.mult).then_inc(o_sb, 1)

                    for g in range(4):
                        seen = 0
                        for what, x in PLAN[g]:
                            if what == "t":
                                low_job(x)
                                if x == sum(TU[:2]) + 1:
                                    o_job(0)
                                seen += 1
                                if seen == 1 and g > 0:
                                    inv_job(g, sbase, rbase + g)
                            elif x[0] == "q":
                                rot_job(BSLOT[x], x[1], qbase)
                            elif x[0] == "s":
                                max_job(x[1], x[2], sbase)
                    inv_job(4, sbase, rbase + 4)
                    o_job(1)
                for pr in range(PAIRS):
                    dve.wait_ge(oh_rdy, b * PAIRS + pr + 1)
                    nc.vector.tensor_tensor(ql[:, pr % 2, :], osb[:, pr, :], qh[:, pr % 2, :].bitcast(F32),
                                            ALU.subtract).then_inc(ol_rdy, 1)
                for i in range(NT):
                    dve.wait_ge(y_ready, b * NT + i + 1)
                    nc.vector.tensor_tensor(xb[:, i, :], banks[:, i, 0:D], xb[:, i, :], ALU.add).then_inc(x2_ready, 1)

        @block.gpsimd
        def _(pool):
            def split(buf, oh, ol, added, high, done, n):
                nc.gpsimd.tensor_tensor(rot1[0:64, buf, :], rot1[0:64, buf, :], rot2[:, buf, :], ALU.add)\
                    .then_inc(added, 1)
                pool.wait_ge(high, n + 1)
                nc.gpsimd.tensor_tensor(ol, rot1[:, buf, :], oh.bitcast(F32), ALU.subtract).then_inc(done, 1)

            nc.gpsimd.memset(ones[:], 1.0).then_inc(l_rep, 1)
            pool.wait_ge(l_rep, 1)
            with pool.Fori(0, B) as b:
                for c in range(NC2):
                    pool.wait_ge(k_rot, b * 2 + c + 1)
                    cols = slice(c * QC, (c + 1) * QC)
                    split(c, kTh[:, cols], kTl[:, cols], k_add, k_high, k_rdy, b * 2 + c)

                def split_job(q, qbase):
                    a, c = UNITS[q % 4]
                    cols = slice(c * QC, (c + 1) * QC)
                    pool.wait_ge(q_rot, qbase + q + 1)
                    split(q % 2, qh[:, a, cols], ql[:, a, cols], q_add, q_high, q_split, qbase + q)

                for q in range(4):
                    split_job(q, b * Q_BATCH)
                with pool.Fori(0, PAIRS) as r:
                    qbase = pool.snap(b * Q_BATCH + r * 4)
                    ubase = pool.snap(b * (PAIRS * 4 + 1) + r * 4)

                    def rep_job(u):
                        a, c = UNITS[u]
                        pool.wait_ge(l_inv, ubase + u + 1)
                        if a == 0:
                            pool.wait_ge(l_ps, rbase_o + c)
                        nc.gpsimd.tensor_tensor(lrep[:, :, 64 * a:64 * a + 64],
                                                linv[:, u % 2, :].unsqueeze(2).to_broadcast([P, 4, 64]),
                                                ones[:].unsqueeze(2).to_broadcast([P, 4, 64]), ALU.mult)\
                            .then_inc(l_rep, 1)

                    rbase_o = pool.snap(b * (PAIRS * 2) + r * 2 + 1)
                    rep_job(0)
                    rep_job(1)
                    rep_job(2)
                    for q in range(4, 7):
                        split_job(q, qbase)
                    rep_job(3)
                    split_job(7, qbase)


def ffn(nc, t, ins, out):
    NG = B
    with ExitStack() as ctx:
        def sb(name, shape, dt=F32):
            return ctx.enter_context(nc.sbuf_tensor(name, shape, dt))

        def sem(name):
            return ctx.enter_context(nc.semaphore(name))

        raw = sb("f_raw", [P, 3, MC * D])
        wth, wtl = sb("wth", [P, KC, 2 * GI], F32R), sb("wtl", [P, KC, 2 * GI], F32R)
        dh, dl = sb("dh", [P, MC, D], F32R), sb("dl", [P, MC, D], F32R)
        mu_raw, mu4 = sb("mu_raw", [P, KC, G, GS]), sb("mu4", [P, KC, G, 32])
        mwh, mwl = sb("mwh", [P, GU], F32R), sb("mwl", [P, GU])
        mw = sb("mw", [P, G, GU], F32R)
        gw_raw = sb("gw_raw", [E, D])
        gwh, gwl = sb("gwh", [P, KC, E], F32R), sb("gwl", [P, KC, E], F32R)
        hl_mask, eid = sb("hl_mask", [P, 2]), sb("eid", [P, 2])
        words = ins["inv_map"].shape[0] // E
        inv_raw = sb("inv_raw", [P, words * E], I32)
        inv_f, inv_n, onehot = sb("inv_f", [P, E]), sb("inv_n", [P, E]), sb("onehot", [P, 2, E])

        x2 = sb("x2", [P, NT, D])
        spot_v = Spots(sb("f_spot_v", [1, 64]))
        xn = raw[:, 0, 0:NT * D].rearrange("p (t d) -> p t d", t=NT)
        xTh, xTl = sb("f_xTh", [P, KC, N], F32R), sb("f_xTl", [P, KC, N], F32R)
        stats, aggr = sb("f_stats", [P, NT, 6]), sb("f_aggr", [P, NT, 2])
        vareps, std, rstd = sb("f_vareps", [P, NT]), sb("f_std", [P, NT]), sb("f_rstd", [P, NT])
        r1, r8 = sb("r1", [P, NT]), sb("r8", [P, NT * G])
        lg, sc, rest, wsel = (raw[:, 1, n * NT * E:(n + 1) * NT * E].rearrange("p (t e) -> p t e", t=NT)
                              for n in range(4))
        top = sb("top", [P, NT, 8])
        wselT = sb("wselT", [P, 4, P])
        soft_h = sb("soft_h", [P, NT * G, GS], F32R)
        sst = raw[:, 2, 0:NT * G * 32].rearrange("p (m s) -> p m s", s=32)
        sT = sb("sT", [P, 2, N], F32R)
        mass = sb("mass", [P, NT, G])
        sg = sb("sg", [P, 4, I])
        act_sb = sb("act_sb", [P, 2, GI])
        aTh, aTl = sb("aTh", [P, 2, MC, P], F32R), sb("aTl", [P, 2, MC, P], F32R)

        banks = ctx.enter_context(nc.psum_tensor("fps", [P, 8, 512], F32))

        loaded, chain = sem("f_loaded"), sem("f_dve_chain")
        w_ps, w_h, w_l = sem("f_w_ps"), sem("f_w_high"), sem("f_w_low")
        mu_rdy, mw_ps, mw_h, mw_rdy = sem("mu_ready"), sem("mw_ps"), sem("mw_high"), sem("mw_ready")
        x_loaded, x_stored = sem("f_x_loaded"), sem("f_x_stored")
        st1, st2, st3, st4 = sem("f_stats_done"), sem("f_aggr_done"), sem("f_vareps_done"), sem("f_std_done")
        xn_ready, xT_ps, xT_h, xT_l = sem("f_xn_ready"), sem("f_xT_ps"), sem("f_xT_h"), sem("f_xT_l")
        lg_ps, lg_sub, lg_exp, w_sel = sem("logits_ps"), sem("logits_shifted"), sem("logits_exp"), sem("w_selected")
        wT_ps, wT_sb, fl_ps, fl_sub, fl_exp = (sem("wselT_ps"), sem("wselT_sb"), sem("flat_ps"), sem("flat_shifted"),
                                               sem("flat_exp"))
        soft_rdy, sT_ps, sT_rdy = sem("soft_ready"), sem("sT_ps"), sem("sT_ready")
        gu_ps, silu_done, a_ready = sem("gate_up_ps"), sem("silu_done"), sem("a_ready")
        aT_ps, aT_h, aT_l, y_ps, o_ready = sem("aT_ps"), sem("aT_high"), sem("aT_low"), sem("y_ps"), sem("out_ready")

        block = ctx.enter_context(nc.Block())
        LOADS = 4 + G + 4 + G
        x2_v = t.x2_dram.rearrange("b (t p) d -> b p t d", p=P)
        out_v = out.rearrange("b (t p) d -> b p t d", p=P)
        raw_w = raw[:].rearrange("p w (m d) -> p w m d", m=MC)
        raw_d = raw[:, 2, :].rearrange("p (k c) -> p k c", k=KC)

        WJOBS = [("w", w, k, m, min(4, MC - m)) for w in range(2) for k in range(KC) for m in range(0, MC, 4)]
        WJOBS += [("d", 0, 0, m, min(2, MC - m)) for m in range(0, MC, 2)]
        WJOBS += [("r", 0, 0, 0, KC)]

        def w_dest(job, hi):
            kind, w, k, m, n = job
            if kind == "w":
                return (wth if hi else wtl)[:, k, w * GI + m * P:w * GI + (m + n) * P]
            if kind == "d":
                return (dh if hi else dl)[:, m:m + n, :].rearrange("p m d -> p (m d)")
            return (gwh if hi else gwl)[:].rearrange("p k e -> p (k e)")

        def w_bank(j):
            kind, _, _, _, n = WJOBS[j]
            width = n * (P if kind == "w" else D if kind == "d" else E)
            return banks[:, j % 6, 0:width]

        @block.sync
        def _(sp):
            for w, name in ((0, "gate_proj_w"), (1, "up_proj_w")):
                sp.dma_start(raw_w[:, w], ins[name].rearrange("g i d -> (g i) d").rearrange("(m p) d -> p m d", p=P))\
                    .then_inc(loaded, 16)
            for g in range(G):
                sp.dma_start(raw_d[:, :, g * I:(g + 1) * I],
                             ins["down_proj_w"][g].rearrange("(k p) i -> p k i", p=P)).then_inc(loaded, 16)
                sp.dma_start(mu_raw[:, :, g, :],
                             ins["mask_up_w"][g].rearrange("(k p) i -> p k i", p=P)).then_inc(loaded, 16)
            sp.dma_start(gw_raw[:], ins["gate_w"]).then_inc(loaded, 16)
            sp.dma_start(hl_mask[:], ins["hl_mask"]).then_inc(loaded, 16)
            sp.dma_start(eid[:], ins["eid"]).then_inc(loaded, 16)
            sp.dma_start(inv_raw[:], ins["inv_map"].partition_broadcast(P)).then_inc(loaded, 16)
            with sp.Fori(0, NG) as b:
                sp.wait_ge(x_stored, b * (16 * NT) + 1)
                sp.dma_start(x2[:], x2_v[bass.ds(b, 1)].rearrange("a p t d -> (a p) t d")).then_inc(x_loaded, 16)
                for i in range(NT):
                    sp.wait_ge(o_ready, b * NT + i + 1)
                    sp.dma_start(out_v[bass.ds(b, 1), :, i, :].rearrange("a p d -> (a p) d"), x2[:, i, :])\
                        .then_inc(x_stored, 16)
            sp.wait_ge(x_stored, B * 16 * NT + 1)

        N_LOADED = 16 * (2 + 2 * G + 4)

        @block.tensor
        def _(pe):
            pe.wait_ge(loaded, N_LOADED)
            for j, (kind, w, k, m, n) in enumerate(WJOBS):
                if j >= 6:
                    pe.wait_ge(w_l, j - 5)
                if kind == "w":
                    for i in range(n):
                        last = nc.tensor.transpose(banks[:, j % 6, i * P:(i + 1) * P],
                                                   raw_w[:, w, m + i, k * P:(k + 1) * P], t.ident[:])
                elif kind == "d":
                    for i in range(n):
                        for kk in range(KC):
                            last = nc.tensor.transpose(banks[:, j % 6, i * D + kk * P:i * D + (kk + 1) * P],
                                                       raw_d[:, kk, (m + i) * P:(m + i + 1) * P], t.ident[:])
                else:
                    for kk in range(KC):
                        last = nc.tensor.transpose(banks[:, j % 6, kk * E:(kk + 1) * E],
                                                   gw_raw[:, kk * P:(kk + 1) * P], t.ident[0:E, 0:E])
                last.then_inc(w_ps, 1)
            pe.wait_ge(w_l, len(WJOBS))
            pe.wait_ge(mu_rdy, 4)
            for q in range(2):
                for gg in range(4):
                    g = 4 * q + gg
                    n = 0
                    for k in range(KC):
                        for part in (wth, wtl):
                            rhs = part[:, k, :].bitcast(F32).rearrange("p (w c) -> p w c", w=2)[:, :, g * I:(g + 1) * I]
                            last = mm(nc, banks[32 * gg:32 * gg + 32, 6 + q, 0:GU].rearrange("p (w c) -> p w c", w=2),
                                      mu4[:, k, g, :], rhs, n == 0, n == 3)
                            n += 1
                last.then_inc(mw_ps, 1)

            with pe.Fori(0, NG) as b:
                for n in range(4):
                    k, g = n // 2, n % 2
                    pe.wait_ge(xn_ready, b * NT + 4 * (g + 1))
                    for i in range(4):
                        last = nc.tensor.transpose(banks[:, n, i * P:(i + 1) * P],
                                                   xn[:, 4 * g + i, k * P:(k + 1) * P], t.ident[:])
                    last.then_inc(xT_ps, 1)
                pe.wait_ge(xT_l, b * 4 + 4)
                for i in range(NT):
                    tok = slice(i * P, (i + 1) * P)
                    for k in range(KC):
                        for n, (x, w) in enumerate(((xTh, gwh), (xTh, gwl), (xTl, gwh))):
                            last = mm(nc, banks[:, 4, i * E:(i + 1) * E], x[:, k, tok], w[:, k, :],
                                      k == 0 and n == 0, k == KC - 1 and n == 2)
                last.then_inc(lg_ps, 1)
                pe.wait_ge(w_sel, b + 1)
                for i in range(4):
                    last = nc.tensor.transpose(banks[:, 5, i * P:(i + 1) * P],
                                               wsel[:, 2 * i:2 * i + 2, :].rearrange("p t e -> p (t e)"), t.ident[:])
                last.then_inc(wT_ps, 1)
                pe.wait_ge(wT_sb, b + 1)
                for i in range(NT):
                    last = mm(nc, banks[:, 6, i * E:(i + 1) * E], wselT[:, i // 2, :], onehot[:, i % 2, :], True, True)
                last.then_inc(fl_ps, 1)
                pe.wait_ge(soft_rdy, b * 4 + 4)
                for n in range(4):
                    q, hh = n // 2, n % 2
                    for i in range(4):
                        tile = 4 * hh + i
                        src = sst[:, tile * G + 4 * q:tile * G + 4 * q + 4, :].rearrange("p g s -> p (g s)")
                        last = nc.tensor.transpose(banks[:, (7, 0, 1, 2)[n], i * P:(i + 1) * P], src, t.ident[:])
                    last.then_inc(sT_ps, 1)
                pe.wait_ge(sT_rdy, b * 4 + 4)
                if True:
                    pe.wait_ge(mw_rdy, 2)

                def gate_up(i, g):
                    n = i * G + g
                    if n >= 4:
                        pe.wait_ge(a_ready, b * (NT * G) + n - 3)
                    tok = slice(i * P, (i + 1) * P)
                    ps = banks[:, g % 4, 0:GU]
                    ps2 = ps.rearrange("p (w c) -> p w c", w=2)

                    def cols(w, k):
                        return w[:, k, :].rearrange("p (w c) -> p w c", w=2)[:, :, g * I:(g + 1) * I]
                    mm(nc, ps, sT[:, g // 4, tok], mw[:, g, :], True, False)
                    for k in range(KC):
                        for j, (x, w) in enumerate(((xTh, wth), (xTh, wtl), (xTl, wth))):
                            last = mm(nc, ps2, x[:, k, tok], cols(w, k), False, k == KC - 1 and j == 2)
                    last.then_inc(gu_ps, 1)

                def transposes(i):
                    pe.wait_ge(a_ready, b * (NT * G) + (i + 1) * G)
                    for q in range(3):
                        if i >= 1:
                            pe.wait_ge(aT_l, b * (NT * 3) + 3 * i + q - 2)
                        for m in range(4 * q, min(4 * q + 4, MC)):
                            last = nc.tensor.transpose(banks[:, 4 + q, (m - 4 * q) * P:(m - 4 * q + 1) * P],
                                                       act_sb[:, i % 2, m * P:(m + 1) * P], t.ident[:])
                        last.then_inc(aT_ps, 1)

                def down(i):
                    if i >= 1:
                        pe.wait_ge(o_ready, b * NT + i)
                    pe.wait_ge(aT_l, b * (NT * 3) + 3 * i + 3)
                    for m in range(MC):
                        for j, (a, w) in enumerate(((aTh, dh), (aTh, dl), (aTl, dh))):
                            last = mm(nc, banks[:, 7, 0:D], a[:, i % 2, m, :], w[:, m, :],
                                      m == 0 and j == 0, m == MC - 1 and j == 2)
                    last.then_inc(y_ps, 1)

                for i in range(NT + 1):
                    for g in range(G):
                        if i < NT:
                            gate_up(i, g)
                        if i >= 1 and g == 2:
                            transposes(i - 1)
                        if i >= 1 and g == 5:
                            down(i - 1)

        @block.scalar
        def _(act):
            for j, job in enumerate(WJOBS):
                act.wait_ge(w_ps, j + 1)
                nc.scalar.copy(w_dest(job, True), w_bank(j)).then_inc(w_h, 1)
            for q in range(2):
                act.wait_ge(mw_ps, q + 1)
                if q >= 1:
                    act.wait_ge(mw_rdy, q)
                nc.scalar.copy(mwh[:], banks[:, 6 + q, 0:GU]).then_inc(mw_h, 1)
            with act.Fori(0, NG) as b:
                act.wait_ge(st3, b + 1)
                nc.scalar.activation(std[:], vareps[:], ACT.Sqrt).then_inc(st4, 1)
                for n in range(4):
                    k, g = n // 2, n % 2
                    act.wait_ge(xT_ps, b * 4 + n + 1)
                    nc.scalar.copy(xTh[:, k, g * QC:(g + 1) * QC], banks[:, n, :]).then_inc(xT_h, 1)
                act.wait_ge(lg_sub, b + 1)
                nc.scalar.activation(sc, lg, ACT.Exp).then_inc(lg_exp, 1)
                act.wait_ge(wT_ps, b + 1)
                nc.scalar.copy(wselT[:].rearrange("p a n -> p (a n)"), banks[:, 5, :]).then_inc(wT_sb, 1)
                act.wait_ge(fl_sub, b + 1)
                nc.scalar.activation(sc, lg, ACT.Exp).then_inc(fl_exp, 1)
                for n in range(4):
                    q, hh = n // 2, n % 2
                    act.wait_ge(sT_ps, b * 4 + n + 1)
                    nc.scalar.copy(sT[:, q, hh * QC:(hh + 1) * QC], banks[:, (7, 0, 1, 2)[n], :]).then_inc(sT_rdy, 1)

                def high(i):
                    for q in range(3):
                        act.wait_ge(aT_ps, b * (NT * 3) + 3 * i + q + 1)
                        if i >= 2 and q == 0:
                            act.wait_ge(y_ps, b * NT + i - 1)
                        n = min(4, MC - 4 * q)
                        nc.scalar.copy(aTh[:, i % 2, 4 * q:4 * q + n, :].rearrange("p m n -> p (m n)"),
                                       banks[:, 4 + q, 0:n * P]).then_inc(aT_h, 1)

                for i in range(NT + 1):
                    for g in range(G):
                        if i < NT:
                            act.wait_ge(gu_ps, b * (NT * G) + i * G + g + 1)
                            nc.scalar.activation(sg[:, g % 4, :], banks[:, g % 4, 0:I], ACT.Silu)\
                                .then_inc(silu_done, 1)
                        if i >= 1 and g == 2:
                            high(i - 1)

        @block.vector
        def _(dve):
            dve.wait_ge(loaded, N_LOADED)
            for c in range(4):
                nc.vector.tensor_copy(mu4[:, :, :, c * GS:(c + 1) * GS], mu_raw[:]).then_inc(mu_rdy, 1)
            nc.vector.memset(spot_v.tensor[:], 0.0).then_inc(x_stored, 1)
            nc.vector.memset(mw[:].bitcast(F32), 0.0)
            nc.vector.tensor_copy(inv_f[:], inv_raw[:].rearrange("p (e w) -> p e w", w=words)[:, :, 0]).then_inc(chain, 1)
            dve.wait_ge(chain, 1)
            nc.vector.tensor_scalar(inv_n[:], inv_f[:], 0.0, float(E), ALU.is_lt, ALU.mult).then_inc(chain, 1)
            dve.wait_ge(chain, 2)
            nc.vector.tensor_tensor(inv_f[:], inv_f[:], inv_n[:], ALU.add).then_inc(chain, 1)
            dve.wait_ge(chain, 3)
            for h in range(2):
                nc.vector.tensor_scalar(onehot[:, h, :], inv_f[:], eid[:, h:h + 1], None, ALU.is_equal)
            for j, job in enumerate(WJOBS):
                dve.wait_ge(w_h, j + 1)
                nc.vector.tensor_tensor(w_dest(job, False), w_bank(j), w_dest(job, True).bitcast(F32),
                                        ALU.subtract).then_inc(w_l, 1)
            for q in range(2):
                dve.wait_ge(mw_h, q + 1)
                nc.vector.tensor_tensor(mwl[:], banks[:, 6 + q, 0:GU], mwh[:].bitcast(F32), ALU.subtract).then_inc(chain, 1)
                dve.wait_ge(chain, 4 + 2 * q)
                nc.vector.tensor_scalar(mwl[:], mwl[:], hl_mask[:, 1:2], None, ALU.mult).then_inc(chain, 1)
                dve.wait_ge(chain, 5 + 2 * q)
                for gg in range(4):
                    rows = slice(32 * gg, 32 * gg + 32)
                    last = nc.vector.scalar_tensor_tensor(out=mw[rows, 4 * q + gg, :], in0=mwh[rows, :].bitcast(F32),
                                                          scalar=hl_mask[rows, 0:1], in1=mwl[rows, :],
                                                          op0=ALU.mult, op1=ALU.add)
                last.then_inc(mw_rdy, 1)
            CH0, CHB = 7, 13

            with dve.Fori(0, NG) as b:
                base = dve.snap(b * CHB)
                count = [0]

                def step(ins_, wait=dve.wait_ge):
                    count[0] += 1
                    ins_.then_inc(chain, 1)
                    wait(chain, base + CH0 + count[0])

                def apart(semaphore, value):
                    vector_waits(nc, spot_v, semaphore, value)

                dve.wait_ge(x_loaded, b * 16 + 16)
                for i in range(NT):
                    nc.vector.bn_stats(stats[:, i, :], x2[:, i, :]).then_inc(st1, 1)
                vector_waits(nc, spot_v, st1, b * NT + NT)
                for i in range(NT):
                    nc.vector.bn_aggr(aggr[:, i, :], stats[:, i, :]).then_inc(st2, 1)
                dve.wait_ge(st2, b * NT + NT)
                nc.vector.tensor_scalar(vareps[:], aggr[:, :, 1], EPS, None, ALU.add).then_inc(st3, 1)
                dve.wait_ge(st4, b + 1)
                step(nc.vector.reciprocal(rstd[:], std[:]))
                for i in range(NT):
                    nc.vector.tensor_scalar(xn[:, i, :], x2[:, i, :], aggr[:, i, 0:1], rstd[:, i:i + 1],
                                            ALU.subtract, ALU.mult).then_inc(xn_ready, 1)
                for n in range(4):
                    k, g = n // 2, n % 2
                    dve.wait_ge(xT_h, b * 4 + n + 1)
                    cols = slice(g * QC, (g + 1) * QC)
                    nc.vector.tensor_tensor(xTl[:, k, cols], banks[:, n, :], xTh[:, k, cols].bitcast(F32),
                                            ALU.subtract).then_inc(xT_l, 1)
                dve.wait_ge(lg_ps, b + 1)
                lg_v = banks[:, 4, :].rearrange("p (t e) -> p t e", t=NT)
                step(nc.vector.tensor_reduce(out=r1[:], in_=lg_v, axis=AX.X, op=ALU.max))
                nc.vector.tensor_tensor(lg, lg_v, r1[:].unsqueeze(2).to_broadcast([P, NT, E]), ALU.subtract)\
                    .then_inc(lg_sub, 1)
                dve.wait_ge(lg_exp, b + 1)
                step(nc.vector.tensor_reduce(out=r1[:], in_=sc, axis=AX.X, op=ALU.add))
                step(nc.vector.reciprocal(r1[:], r1[:]))
                step(nc.vector.tensor_tensor(sc, sc, r1[:].unsqueeze(2).to_broadcast([P, NT, E]), ALU.mult), apart)
                for i in range(NT):
                    last = nc.vector.max(out=top[:, i, :], in_=sc[:, i, :])
                step(last, apart)
                for i in range(NT):
                    last = nc.vector.match_replace(out=rest[:, i, :], in_to_replace=top[:, i, :], in_values=sc[:, i, :],
                                                   imm_value=0.0)
                step(last)
                nc.vector.tensor_tensor(wsel, sc, rest, ALU.subtract).then_inc(w_sel, 1)
                dve.wait_ge(fl_ps, b + 1)
                fl = banks[:, 6, :].rearrange("p (m s) -> p m s", s=GS)
                lgf = lg.rearrange("p t (g s) -> p (t g) s", s=GS)
                scf = sc.rearrange("p t (g s) -> p (t g) s", s=GS)
                nc.vector.tensor_reduce(out=mass[:].rearrange("p t g -> p (t g)"), in_=fl, axis=AX.X, op=ALU.add)
                step(nc.vector.tensor_scalar(lgf, fl, 0.0, -1.0e9, ALU.is_equal, ALU.mult))
                step(nc.vector.tensor_tensor(lgf, fl, lgf, ALU.add))
                step(nc.vector.tensor_reduce(out=r8[:], in_=lgf, axis=AX.X, op=ALU.max))
                nc.vector.tensor_tensor(lgf, lgf, r8[:].unsqueeze(2).to_broadcast([P, NT * G, GS]), ALU.subtract)\
                    .then_inc(fl_sub, 1)
                dve.wait_ge(fl_exp, b + 1)
                step(nc.vector.tensor_reduce(out=r8[:], in_=scf, axis=AX.X, op=ALU.add))
                step(nc.vector.reciprocal(r8[:], r8[:]))
                step(nc.vector.tensor_tensor(scf, scf, r8[:].unsqueeze(2).to_broadcast([P, NT * G, GS]), ALU.mult))
                assert count[0] == CHB, count
                nc.vector.tensor_copy(soft_h[:], scf).then_inc(soft_rdy, 1)
                dve.wait_ge(soft_rdy, b * 4 + 1)
                nc.vector.tensor_copy(sst.rearrange("p m (r h s) -> p m r h s", r=2, h=2)[:, :, :, 0, :],
                                      soft_h[:].bitcast(F32).unsqueeze(2).to_broadcast([P, NT * G, 2, GS])).then_inc(soft_rdy, 1)
                for r in range(2):
                    nc.vector.tensor_tensor(sst[:, :, (2 * r + 1) * GS:(2 * r + 2) * GS], scf, soft_h[:].bitcast(F32),
                                            ALU.subtract).then_inc(soft_rdy, 1)

                def low(i):
                    for q in range(3):
                        dve.wait_ge(aT_h, b * (NT * 3) + 3 * i + q + 1)
                        n = min(4, MC - 4 * q)
                        nc.vector.tensor_tensor(aTl[:, i % 2, 4 * q:4 * q + n, :].rearrange("p m n -> p (m n)"),
                                                banks[:, 4 + q, 0:n * P],
                                                aTh[:, i % 2, 4 * q:4 * q + n, :].rearrange("p m n -> p (m n)").bitcast(F32),
                                                ALU.subtract).then_inc(aT_l, 1)

                for i in range(NT + 1):
                    for g in range(G):
                        if i < NT:
                            dve.wait_ge(silu_done, b * (NT * G) + i * G + g + 1)
                            nc.vector.scalar_tensor_tensor(out=act_sb[:, i % 2, g * I:(g + 1) * I],
                                                           in0=banks[:, g % 4, I:GU], scalar=mass[:, i, g:g + 1],
                                                           in1=sg[:, g % 4, :], op0=ALU.mult, op1=ALU.mult)\
                                .then_inc(a_ready, 1)
                        if i >= 1 and g == 2:
                            low(i - 1)
                        if i >= 1 and g == 7:
                            dve.wait_ge(y_ps, b * NT + i)
                            nc.vector.tensor_tensor(x2[:, i - 1, :], banks[:, 7, 0:D], x2[:, i - 1, :], ALU.add)\
                                .then_inc(o_ready, 1)


class Shared:
    pass


def build(nc, ins, out):
    with ExitStack() as ctx:
        t = Shared()
        t.wq_dram = nc.dram_tensor("wq_scratch", [PAIRS + 1, P, 2, 2, 192], F32, kind="Internal").ap()
        t.x2_dram = nc.dram_tensor("x2_scratch", [B, N, D], F32, kind="Internal").ap()
        t.ident = ctx.enter_context(nc.sbuf_tensor("ident", [P, P], F32))
        with ExitStack() as at:
            def sb(name, shape, dt=F32):
                return at.enter_context(nc.sbuf_tensor(name, shape, dt))
            t.ident_b, t.mask_b = sb("ident_b", [P, P], BF16), sb("mask_b", [P, P], BF16)
            t.cosT, t.sinT = sb("cosT", [P, N]), sb("sinT", [64, N])
            t.wk = sb("wk", [P, 2, KC, 192], F32R)
            t.wqa = sb("wqa", [P, 2, KC, P], F32R)
            t.w2h, t.w2l = sb("w2h", [P, PAIRS, D], F32R), sb("w2l", [P, PAIRS, D], F32R)
            attention_weights(nc, t, ins)
            attention(nc, t, ins)
        ffn(nc, t, ins, out)


def constants():
    j = np.arange(ROPE // 2)
    theta = (10000.0 ** (-2.0 * j / ROPE)).astype(np.float32)
    ang = (np.arange(N, dtype=np.float32)[:, None] * theta[None, :]).astype(np.float64)
    cos, sin = np.cos(ang).T.astype(np.float32), np.sin(ang).T.astype(np.float32)
    p = np.arange(P)
    return {
        "ident": np.eye(P, dtype=np.float32),
        "mask": np.where(p[None, :] > p[:, None], NEG, 0.0).astype(np.float32),
        "cos": np.ascontiguousarray(np.concatenate([cos, cos, np.ones((64, N), np.float32)])),
        "sin": np.ascontiguousarray(np.concatenate([-sin, sin])),
        "hl_mask": np.stack([(p % 32 < 16), (p % 32 >= 16)], 1).astype(np.float32),
        "eid": np.stack([np.where(p // 64 == h, p % 64, -1) for h in range(2)], 1).astype(np.float32),
    }


def kernel(L0_attn_x, L0_attn_Wqa, L0_attn_Wqb, L0_attn_Wkva, L0_attn_Wkvb, L0_attn_Wout, L0_ffn_gate_w,
           L0_ffn_mask_up_w, L0_ffn_gate_proj_w, L0_ffn_up_proj_w, L0_ffn_down_proj_w, L0_ffn_inv_map):
    import concourse.bacc as bacc
    from concourse.bass_utils import run_bass_kernel_spmd

    nc = bacc.Bacc("TRN2", target_bir_lowering=False, num_devices=1)
    arrays = {"x": L0_attn_x, "Wqa": L0_attn_Wqa, "Wqb": L0_attn_Wqb, "Wkva": L0_attn_Wkva, "Wkvb": L0_attn_Wkvb,
              "Wout": L0_attn_Wout, "gate_w": L0_ffn_gate_w, "mask_up_w": L0_ffn_mask_up_w,
              "gate_proj_w": L0_ffn_gate_proj_w, "up_proj_w": L0_ffn_up_proj_w, "down_proj_w": L0_ffn_down_proj_w}
    arrays = {k: np.ascontiguousarray(v) for k, v in arrays.items()}
    arrays["inv_map"] = np.ascontiguousarray(L0_ffn_inv_map).reshape(-1).view(np.int32)
    arrays.update(constants())
    ins, feed = {}, {}
    for k, v in arrays.items():
        ins[k] = nc.dram_tensor(f"in_{k}", v.shape, mybir.dt.from_np(v.dtype), kind="ExternalInput").ap()
        feed[f"in_{k}"] = v
    out = nc.dram_tensor("out", (B, N, D), F32, kind="ExternalOutput").ap()
    build(nc, ins, out)
    r = run_bass_kernel_spmd(nc, [feed], core_ids=[0])
    return r.results[0]["out"]
```

```python
import numpy as np
import concourse.bass as bass
from concourse import mybir
from contextlib import ExitStack

F32 = mybir.dt.float32
F32R = mybir.dt.float32r
BF16 = mybir.dt.bfloat16
I32 = mybir.dt.int32
ALU = mybir.AluOpType
ACT = mybir.ActivationFunctionType
AX = mybir.AxisListType

B, N, D = 4, 1024, 256
H, NOPE, VD, ROPE = 16, 128, 128, 64
QH = NOPE + ROPE
RANK = 64
P = 128
KC = D // P
NT = N // P
PAIRS = H // 2
SCALE = 1.0 / np.sqrt(QH)
EPS = 1e-5
NEG = -3.0e38
G, GS, I, E, TOPK = 8, 8, 176, 64, 8
GI = G * I
MC = GI // P
GU = 2 * I
QC = 512
NC2 = N // QC
PW = [[(4 * c + j + 1) * P for j in range(4)] for c in range(NC2)]
POFF = [[sum(PW[c][:j]) for j in range(4)] for c in range(NC2)]
PBUF = sum(PW[1])

UNITS = [(0, 0), (1, 0), (0, 1), (1, 1)]
S_BATCH = 4 + 16 * PAIRS
Q_BATCH = 4 + 4 * PAIRS
TU = [4, 4, 8, 8]
T_PAIR = sum(TU)


def mm(nc, out, lhsT, rhs, start, stop):
    return nc.tensor.matmul(out, lhsT, rhs, start=start, stop=stop, skip_group_check=True)


class Spots:

    def __init__(self, tensor):
        self.tensor, self.n = tensor, 0

    def next(self):
        self.n += 1
        return self.tensor[:, self.n:self.n + 1]


def vector_waits(nc, spots, semaphore, value):
    nc.vector.wait_ge(semaphore, value)
    nc.vector.memset(spots.next(), 0.0)


def attention_weights(nc, t, ins):
    with ExitStack() as ctx:
        def sb(name, shape, dt=F32):
            return ctx.enter_context(nc.sbuf_tensor(name, shape, dt))

        def sem(name):
            return ctx.enter_context(nc.semaphore(name))

        wqb = sb("wqb", [P, H * QH])
        wkvb = sb("wkvb", [P, H * (NOPE + VD)])
        wout = sb("wout", [P, H, D])
        wqa = sb("wqa_raw", [P, KC, RANK])
        wkva = sb("wkva_raw", [P, KC, RANK + ROPE])
        mask = sb("mask", [P, P])
        wT = sb("wT", [P, H, 3 * P])
        wq = sb("wq_all", [P, PAIRS, 2, 2, 192], F32R)
        ps = ctx.enter_context(nc.psum_tensor("wps", [P, 8, 512], F32))

        heads_loaded, plain_loaded = sem("head_weights_loaded"), sem("plain_weights_loaded")
        out_loaded, tables_loaded = sem("wout_loaded"), sem("tables_loaded")
        heads_T = sem("heads_transposed")
        heads_T_sb = sem("heads_transposed_in_sbuf")
        prod = sem("head_products")
        prod_h = sem("head_products_high")
        prod_done = sem("head_products_done")
        plain_h = sem("plain_high")
        plain_done = sem("plain_done")
        stored = sem("wq_stored")

        block = ctx.enter_context(nc.Block())
        raw_pe = wqb[:].rearrange("p (r a c) -> p r a c", r=PAIRS, a=2)[:, :, :, NOPE:QH]\
                       .rearrange("p r a (j e) -> p r a j e", e=2)
        raw_kpe = wkva[:, :, RANK:].rearrange("p k (j e) -> p k j e", e=2)

        @block.sync
        def _(sp):
            sp.dma_start(t.ident[:], ins["ident"]).then_inc(heads_loaded, 16)
            for r in (0, 64):
                sp.dma_start(wqb[r:r + 64, :], ins["Wqb"]).then_inc(heads_loaded, 16)
                sp.dma_start(wkvb[r:r + 64, :], ins["Wkvb"]).then_inc(heads_loaded, 16)
            sp.dma_start(wout[:], ins["Wout"].rearrange("(h p) n -> p h n", p=P)).then_inc(out_loaded, 16)
            sp.dma_start(wqa[:], ins["Wqa"].rearrange("(k p) n -> p k n", p=P)).then_inc(plain_loaded, 16)
            sp.dma_start(wkva[:], ins["Wkva"].rearrange("(k p) n -> p k n", p=P)).then_inc(plain_loaded, 16)
            sp.dma_start(mask[:], ins["mask"]).then_inc(tables_loaded, 16)
            sp.dma_start(t.cosT[:], ins["cos"]).then_inc(tables_loaded, 16)
            sp.dma_start(t.sinT[:], ins["sin"]).then_inc(tables_loaded, 16)
            sp.dma_start(t.xb[:], ins["x"][0].rearrange("(t p) d -> p t d", p=P)).then_inc(t.x_loaded, 16)
            sp.wait_ge(plain_done, 1)
            for r in range(PAIRS + 1):
                sp.wait_ge(prod_done, min(2 * r + 2, H))
                sp.dma_start(t.wq_dram[r], wq[:, r % PAIRS].bitcast(F32)).then_inc(stored, 16)
            sp.wait_ge(stored, 16 * (PAIRS + 1))

        @block.tensor
        def _(pe):
            pe.wait_ge(heads_loaded, 16 * 5)
            for h in range(H):
                if h >= 8:
                    pe.wait_ge(heads_T_sb, h - 7)
                srcs = [wqb[:, h * QH:h * QH + NOPE], wkvb[:, h * 256:h * 256 + NOPE],
                        wkvb[:, h * 256 + NOPE:(h + 1) * 256]]
                for k, src in enumerate(srcs):
                    last = nc.tensor.transpose(ps[:, h % 8, k * P:(k + 1) * P], src, t.ident[:])
                last.then_inc(heads_T, 1)
            pe.wait_ge(out_loaded, 16)
            for h in range(H):
                pe.wait_ge(heads_T_sb, min(h + 9, H))
                if h >= 8:
                    pe.wait_ge(prod_done, h - 7)
                mm(nc, ps[:, h % 8, 0:RANK], wT[:, h, 0:P], wT[:, h, P:P + RANK], True, True)
                mm(nc, ps[:, h % 8, RANK:RANK + D], wT[:, h, 2 * P:3 * P], wout[:, h, :], True, True)\
                    .then_inc(prod, 1)

        @block.scalar
        def _(act):
            for h in range(H):
                act.wait_ge(heads_T, h + 1)
                nc.scalar.copy(wT[:, h, :], ps[:, h % 8, 0:3 * P]).then_inc(heads_T_sb, 1)
            act.wait_ge(heads_loaded, 16 * 5)
            act.wait_ge(plain_loaded, 32)
            for k in (0, 1):
                c = slice(32 * k, 32 * k + 32)
                cy = slice(P + 32 * k, P + 32 * k + 32)
                for a in range(2):
                    nc.scalar.mul(wq[:, :, 0, a, c], raw_pe[:, :, a, :, k], SCALE)
                    nc.scalar.mul(wq[:, :, 0, a, cy], raw_pe[:, :, a, :, 1 - k], SCALE)
                nc.scalar.copy(t.wk[:, 0, :, c], raw_kpe[:, :, :, k])
                nc.scalar.copy(t.wk[:, 0, :, cy], raw_kpe[:, :, :, 1 - k])
                nc.scalar.copy(t.wqa[:, 0, :, 64 * k:64 * k + 64], wqa[:])
            nc.scalar.copy(t.wk[:, 0, :, 64:128], wkva[:, :, 0:RANK]).then_inc(plain_h, 1)
            for h in range(H):
                r = 64 * (h % 2)
                act.wait_ge(prod, h + 1)
                nc.scalar.mul(wq[:, h // 2, 0, h % 2, 64:128], ps[:, h % 8, 0:RANK], SCALE)
                nc.scalar.copy(t.w2h[r:r + 64, h // 2, :], ps[r:r + 64, h % 8, RANK:RANK + D]).then_inc(prod_h, 1)

        @block.vector
        def _(dve):
            dve.wait_ge(heads_loaded, 16 * 5)
            dve.wait_ge(plain_loaded, 32)
            dve.wait_ge(tables_loaded, 48)
            nc.vector.tensor_copy(t.ident_b[:], t.ident[:])
            nc.vector.tensor_copy(t.mask_b[:], mask[:])
            dve.wait_ge(plain_h, 1)
            for k in (0, 1):
                c = slice(32 * k, 32 * k + 32)
                cy = slice(P + 32 * k, P + 32 * k + 32)
                for a in range(2):
                    for cols, e in ((c, k), (cy, 1 - k)):
                        nc.vector.scalar_tensor_tensor(out=wq[:, :, 1, a, cols], in0=raw_pe[:, :, a, :, e],
                                                       scalar=float(SCALE), in1=wq[:, :, 0, a, cols].bitcast(F32),
                                                       op0=ALU.mult, op1=ALU.subtract)
                for cols, e in ((c, k), (cy, 1 - k)):
                    nc.vector.tensor_tensor(t.wk[:, 1, :, cols], raw_kpe[:, :, :, e],
                                            t.wk[:, 0, :, cols].bitcast(F32), ALU.subtract)
                nc.vector.tensor_tensor(t.wqa[:, 1, :, 64 * k:64 * k + 64], wqa[:],
                                        t.wqa[:, 0, :, 64 * k:64 * k + 64].bitcast(F32), ALU.subtract)
            nc.vector.tensor_tensor(t.wk[:, 1, :, 64:128], wkva[:, :, 0:RANK],
                                    t.wk[:, 0, :, 64:128].bitcast(F32), ALU.subtract).then_inc(plain_done, 1)
            for h in range(H):
                r = 64 * (h % 2)
                dve.wait_ge(prod_h, h + 1)
                cols = wq[:, h // 2, 0, h % 2, 64:128]
                nc.vector.scalar_tensor_tensor(out=wq[:, h // 2, 1, h % 2, 64:128], in0=ps[:, h % 8, 0:RANK],
                                               scalar=float(SCALE), in1=cols.bitcast(F32),
                                               op0=ALU.mult, op1=ALU.subtract)
                nc.vector.tensor_tensor(t.w2l[r:r + 64, h // 2, :], ps[r:r + 64, h % 8, RANK:RANK + D],
                                        t.w2h[r:r + 64, h // 2, :].bitcast(F32), ALU.subtract).then_inc(prod_done, 1)


def attention(nc, t, ins):
    with ExitStack() as ctx:
        def sb(name, shape, dt=F32):
            return ctx.enter_context(nc.sbuf_tensor(name, shape, dt))

        def sem(name):
            return ctx.enter_context(nc.semaphore(name))

        xb = t.xb
        kTh, kTl = sb("kTh", [P, N], F32R), sb("kTl", [P, N], F32R)
        vh, vl = sb("vh", [P, NT, 192], F32R), sb("vl", [P, NT, 192], F32R)
        xq = sb("xq", [P, N], F32R)
        wqs = sb("wqs", [P, 2, 2, 192], F32R)
        qh, ql = sb("qh", [P, 2, N], F32R), sb("ql", [P, 2, N], F32R)
        psb = sb("psb", [P, 2, PBUF])
        pTh, pTl = sb("pTh", [P, 3, QC], F32R), sb("pTl", [P, 3, QC], F32R)
        osb = sb("osb", [P, PAIRS, N])
        rot1, rot2 = sb("rot1", [P, 2, QC]), sb("rot2", [64, 2, QC])
        nmax, lsum, linv = sb("nmax", [P, 2, 4]), sb("lsum", [P, 2, 4]), sb("linv", [P, 2, 4])
        lrep, ones = sb("lrep", [P, 4, P]), sb("ones", [P, 4])
        linv_b = sb("linv_b", [P, 2, QC])
        stats, aggr = sb("stats", [P, NT, 6]), sb("aggr", [P, NT, 2])
        vareps, std, rstd = sb("vareps", [P, NT]), sb("std", [P, NT]), sb("rstd", [P, NT])
        spot_v = Spots(sb("spot_v", [1, 64]))
        xn, x2b = (psb[:, n, 0:NT * D].rearrange("p (t d) -> p t d", t=NT) for n in range(2))

        banks = ctx.enter_context(nc.psum_tensor("aps", [P, 8, 512], F32))
        sps = banks[:, 0:4, :].rearrange("p (s b) n -> p s b n", s=2)
        tps = banks[:, 4:7, :]
        ops = banks[:, 7, :]

        x_loaded, x_again, x_stored = t.x_loaded, sem("x_loaded_again"), sem("x_stored")
        zeroed = sem("v_zeroed")
        st1, st2, st3, st4, st5 = (sem("stats_done"), sem("aggr_done"), sem("vareps_done"), sem("std_done"),
                                   sem("rstd_done"))
        xn_ready = sem("xn_ready")
        xT_ps, xT_h, xT_l = sem("xT_ps"), sem("xT_h"), sem("xT_l")
        xq_ps, xq_h, xq_rdy = sem("xq_ps"), sem("xq_h"), sem("xq_ready")
        k_ps, k_rot, k_add, k_high, k_rdy = (sem("k_ps"), sem("k_rotated"), sem("k_added"), sem("k_high"),
                                             sem("k_ready"))
        v_ps, v_h, v_rdy = sem("v_ps"), sem("v_h"), sem("v_ready")
        wq_loaded = sem("wq_loaded")
        q_ps, q_rot, q_add, q_high, q_split = (sem("q_ps"), sem("q_rotated"), sem("q_added"), sem("q_high"),
                                               sem("q_split"))
        s_ready, m_ready, e_done = sem("scores_ready"), sem("max_ready"), sem("exp_done")
        l_inv, l_rep, l_ps, l_sb = (sem("rowsums_inverted"), sem("inverses_repeated"), sem("inverses_ps"),
                                    sem("inverses_sb"))
        t_ready, t_high, t_low, pv_done = sem("pT_ready"), sem("pT_high"), sem("pT_low"), sem("pv_done")
        o_sb = sem("o_in_sbuf")
        oh_rdy, ol_rdy, y_used, y_ready, x2_ready = (sem("o_high"), sem("o_low"), sem("o_projected"),
                                                     sem("y_ready"), sem("x2_ready"))

        block = ctx.enter_context(nc.Block())
        x_v = ins["x"].rearrange("b (t p) d -> b p t d", p=P)
        x2_v = t.x2_dram.rearrange("b (t p) d -> b p t d", p=P)

        def s_(v, j):
            return ("s", v, j)

        PROLOGUE = [("q", q, 0) for q in range(4)] + [s_(0, j) for j in range(4)]
        BODY = [[s_(1, j) for j in range(4)],
                [s_(2, 0), s_(2, 1), s_(2, 2), ("l", 0, 0), s_(2, 3)],
                [s_(3, 0), ("q", 4, 0), s_(3, 1), ("q", 5, 0), s_(3, 2), ("q", 6, 0), s_(3, 3)],
                [s_(4, 0), s_(4, 1), ("q", 7, 0), ("l", 1, 0), s_(4, 2), s_(4, 3)]]
        FLAT = [x for g in BODY for x in g]
        assert len(FLAT) % 2 == 0 and len(PROLOGUE) % 2 == 0 and T_PAIR % 3 == 0
        SLOT = {x: n % 2 for n, x in enumerate(PROLOGUE)}
        BEFORE = {x: PROLOGUE[n - 2] if n >= 2 else None for n, x in enumerate(PROLOGUE)}
        BSLOT = {x: n % 2 for n, x in enumerate(FLAT)}
        BBEFORE = {}
        for n, x in enumerate(FLAT):
            if n >= 2:
                BBEFORE[x] = FLAT[n - 2]
            else:
                k, v, j = FLAT[n - 2]
                BBEFORE[x] = (k, v - 4, j)

        def s_index(v, j):
            return 4 * v + j

        def plan(g):
            first = sum(TU[:g])
            n = TU[g]
            ts = [("t", first + k) for k in range(n)]
            xs = [("x", x) for x in BODY[g]]
            out = xs[:2]
            rest = xs[2:]
            parts = len(rest) + 1
            for k in range(parts):
                out += ts[k * n // parts:(k + 1) * n // parts]
                out += rest[k:k + 1]
            return out

        PLAN = [plan(g) for g in range(4)]

        def t_unit(n):
            u = next(u for u in range(4) if n < sum(TU[:u + 1]))
            return u, n - sum(TU[:u])

        def t_cols(n):
            u, kb = t_unit(n)
            return max(0, kb - 4 * UNITS[u][1]) * P

        @block.sync
        def _(sp):
            def batch(b, more):
                sp.dma_start(wqs[:].bitcast(F32), t.wq_dram[0]).then_inc(wq_loaded, 16)
                if more:
                    following = sp.snap(b + 1)
                    sp.wait_ge(xn_ready, b * NT + NT)
                    sp.dma_start(xb[:], x_v[bass.ds(following, 1)].rearrange("a p t d -> (a p) t d"))\
                        .then_inc(x_loaded, 16)
                with sp.Fori(0, PAIRS) as r:
                    sp.wait_ge(q_ps, b * Q_BATCH + r * 4 + 4)
                    sp.dma_start(wqs[:].bitcast(F32), t.wq_dram[bass.ds(r + 1, 1)].rearrange("a p l h c -> (a p) l h c"))\
                        .then_inc(wq_loaded, 16)
                sp.wait_ge(t_ready, b * (PAIRS * T_PAIR) + PAIRS * T_PAIR)
                sp.dma_start(x2b, x_v[bass.ds(b, 1)].rearrange("a p t d -> (a p) t d")).then_inc(x_again, 16)
                sp.wait_ge(x2_ready, b * NT + 2 * NT)
                sp.dma_start(x2_v[bass.ds(b, 1)].rearrange("a p t d -> (a p) t d"), x2b).then_inc(x_stored, 16)

            with sp.Fori(0, B - 1) as b:
                batch(b, True)
            batch(B - 1, False)
            sp.wait_ge(x_stored, 16 * B + 1)

        @block.tensor
        def _(pe):
            def batch(b, more):
                for n in range(4):
                    k, g = n // 2, n % 2
                    pe.wait_ge(xn_ready, b * NT + 4 * (g + 1))
                    pe.wait_ge(x2_ready, b * NT + n + 1)
                    for i in range(4):
                        last = nc.tensor.transpose(banks[:, n, i * P:(i + 1) * P],
                                                   xn[:, 4 * g + i, k * P:(k + 1) * P], t.ident[:])
                    last.then_inc(xT_ps, 1)
                pe.wait_ge(xT_l, b * 4 + 4)
                pe.wait_ge(x2_ready, b * NT + NT)

                def project(out, w, cols, c):
                    for k in range(KC):
                        for n, (wp, xp) in enumerate(((0, qh), (0, ql), (1, qh))):
                            last = mm(nc, out, w[:, wp, k, cols], xp[:, k, c * QC:(c + 1) * QC],
                                      k == 0 and n == 0, k == KC - 1 and n == 2)
                    return last

                for c in range(NC2):
                    project(banks[:, 4 + c, :], t.wqa, slice(0, P), c).then_inc(xq_ps, 1)
                for c in range(NC2):
                    kb = (6, 0)[c]
                    project(banks[:, kb, :], t.wk, slice(0, P), c)
                    project(banks[0:64, kb + 1, :], t.wk, slice(P, 192), c).then_inc(k_ps, 1)
                for g in range(2):
                    for i in range(4):
                        tok = slice((4 * g + i) * P, (4 * g + i + 1) * P)
                        out = banks[:, 2 + g, i * 64:(i + 1) * 64]
                        for k in range(KC):
                            for n, (xp, wp) in enumerate(((qh, 0), (qh, 1), (ql, 0))):
                                last = mm(nc, out, xp[:, k, tok], t.wk[:, wp, k, 64:128],
                                          k == 0 and n == 0, k == KC - 1 and n == 2)
                    last.then_inc(v_ps, 1)

                def q_job(slot, q, base):
                    a, c = UNITS[q % 4]
                    if q % 4 == 0:
                        pe.wait_ge(wq_loaded, base)
                    rhs = xq[:, c * QC:(c + 1) * QC]
                    for wp in range(2):
                        mm(nc, sps[:, slot, 0, :], wqs[:, wp, a, 0:P], rhs, wp == 0, wp == 1)
                    for wp in range(2):
                        last = mm(nc, sps[0:64, slot, 1, :], wqs[:, wp, a, P:192], rhs, wp == 0, wp == 1)
                    last.then_inc(q_ps, 1)

                def s_job(slot, v, j, qbase):
                    a, c = UNITS[v % 4]
                    if j == 0:
                        pe.wait_ge(q_split, qbase + v + 1)
                    w = PW[c][j]
                    tok = slice((4 * c + j) * P, (4 * c + j + 1) * P)
                    segs = [(s, min(QC, w - s)) for s in range(0, w, QC)]
                    for n, (q, ks) in enumerate(((qh, (kTh, kTl)), (ql, (kTh,)))):
                        for i, (s, m) in enumerate(segs):
                            for kk, kt in enumerate(ks):
                                diag = s + m == w
                                last = mm(nc, sps[:, slot, i, 0:m], q[:, a, tok], kt[:, s:s + m],
                                          n == 0 and kk == 0, n == 1 and not diag)
                    i = len(segs) - 1
                    m = segs[i][1]
                    mm(nc, sps[:, slot, i, m - P:m], t.ident_b[:], t.mask_b[:], False, True).then_inc(s_ready, 1)

                def slot_free(before, sbase, qbase, obase=None):
                    if before is None:
                        return
                    kind, v, j = before
                    if kind == "s":
                        pe.wait_ge(e_done, sbase + s_index(v, j) + 1)
                    elif kind == "q":
                        pe.wait_ge(q_rot, qbase + v + 1)
                    else:
                        pe.wait_ge(l_sb, obase + v + 1)

                sb0, qb0 = b * S_BATCH, b * Q_BATCH
                pe.wait_ge(xq_rdy, b * 2 + 2)
                pe.wait_ge(k_rdy, b * 2 + 2)
                pe.wait_ge(v_rdy, b * 2 + 2)
                for x in PROLOGUE:
                    slot_free(BEFORE[x], sb0, qb0)
                    if x[0] == "q":
                        q_job(SLOT[x], x[1], b * (16 * (PAIRS + 1)) + 16)
                    else:
                        s_job(SLOT[x], x[1], x[2], qb0)

                with pe.Fori(0, PAIRS) as r:
                    sbase = pe.snap(b * S_BATCH + r * 16)
                    qbase = pe.snap(b * Q_BATCH + r * 4)
                    wbase = pe.snap(b * (16 * (PAIRS + 1)) + r * 16 + 32)
                    tbase = pe.snap(b * (PAIRS * T_PAIR) + r * T_PAIR)
                    obase = pe.snap(b * (PAIRS * 2) + r * 2)

                    def t_job(n):
                        u, kb = t_unit(n)
                        if kb == 0:
                            pe.wait_ge(e_done, sbase + 4 * u + 4)
                        pe.wait_ge(t_low, tbase + n + 1)
                        for j in range(t_cols(n) // P, 4):
                            off = POFF[UNITS[u][1]][j] + kb * P
                            last = nc.tensor.transpose(tps[:, n % 3, j * P:(j + 1) * P],
                                                       psb[:, u % 2, off:off + P], t.ident[:])
                        last.then_inc(t_ready, 1)

                    def pv_job(n):
                        u, kb = t_unit(n)
                        a, c = UNITS[u]
                        if a == 0 and kb == 0:
                            pe.wait_ge(o_sb, obase + c + 1)
                        pe.wait_ge(t_low, tbase + n + 4)
                        s = t_cols(n)
                        cols = slice(64, 192) if a == 0 else slice(0, P)
                        for i, (v, pt) in enumerate(((vh, pTh), (vl, pTh), (vh, pTl))):
                            last = mm(nc, ops[:, s:QC], v[:, kb, cols], pt[:, n % 3, s:QC],
                                      a == 0 and kb == 0 and i == 0, a == 1 and kb == TU[u] - 1 and i == 2)
                        last.then_inc(pv_done, 1)

                    pending = []
                    for g in range(4):
                        for what, x in PLAN[g]:
                            if what == "x":
                                slot_free(BBEFORE[x], sbase, qbase, obase)
                                if x[0] == "q":
                                    q_job(BSLOT[x], x[1], wbase)
                                elif x[0] == "l":
                                    pe.wait_ge(l_rep, 2 * obase + 2 * x[1] + 3)
                                    for j in range(4):
                                        last = nc.tensor.transpose(sps[:, BSLOT[x], 0, j * P:(j + 1) * P],
                                                                   lrep[:, j, :], t.ident[:])
                                    last.then_inc(l_ps, 1)
                                else:
                                    s_job(BSLOT[x], x[1], x[2], qbase)
                            else:
                                t_job(x)
                                pending.append(x)
                                if len(pending) > 2:
                                    pv_job(pending.pop(0))
                    for n in pending:
                        pv_job(n)

                pe.wait_ge(e_done, b * S_BATCH + S_BATCH)
                pe.wait_ge(o_sb, b * (PAIRS * 2) + PAIRS * 2 + 1)
                for pr in range(PAIRS):
                    pe.wait_ge(ol_rdy, b * PAIRS + pr + 1)
                    for i in range(NT):
                        tok = slice(i * P, (i + 1) * P)
                        for n, (o, w) in enumerate(((qh, t.w2h), (qh, t.w2l), (ql, t.w2h))):
                            last = mm(nc, banks[:, i, 0:D], o[:, pr % 2, tok], w[:, pr, :],
                                      pr == 0 and n == 0, pr == PAIRS - 1 and n == 2)
                        if pr == PAIRS - 1:
                            last.then_inc(y_ready, 1)
                    if pr < PAIRS - 1:
                        last.then_inc(y_used, 1)

            with pe.Fori(0, B - 1) as b:
                batch(b, True)
            batch(B - 1, False)

        @block.scalar
        def _(act):
            def root(b):
                act.wait_ge(st3, b + 1)
                nc.scalar.activation(std[:], vareps[:], ACT.Sqrt).then_inc(st4, 1)

            def batch(b, more):
                for n in range(4):
                    k, g = n // 2, n % 2
                    act.wait_ge(xT_ps, b * 4 + n + 1)
                    nc.scalar.copy(qh[:, k, g * QC:(g + 1) * QC], banks[:, n, :]).then_inc(xT_h, 1)
                for c in range(NC2):
                    act.wait_ge(xq_ps, b * 2 + c + 1)
                    nc.scalar.copy(xq[:, c * QC:(c + 1) * QC], banks[:, 4 + c, :]).then_inc(xq_h, 1)
                for g in range(2):
                    act.wait_ge(v_ps, b * 2 + g + 1)
                    if g == 0:
                        act.wait_ge(zeroed, 2)
                    nc.scalar.copy(vh[:, 4 * g:4 * g + 4, 64:128],
                                   banks[:, 2 + g, 0:256].rearrange("p (t c) -> p t c", t=4)).then_inc(v_h, 1)

                for c in range(NC2):
                    cols = slice(c * QC, (c + 1) * QC)
                    act.wait_ge(k_add, b * 2 + c + 1)
                    nc.scalar.copy(kTh[:, cols], rot1[:, c, :]).then_inc(k_high, 1)

                def q_high_job(q, qbase):
                    a, c = UNITS[q % 4]
                    act.wait_ge(q_add, qbase + q + 1)
                    nc.scalar.copy(qh[:, a, c * QC:(c + 1) * QC], rot1[:, q % 2, :]).then_inc(q_high, 1)

                def exp_job(v, j, sbase):
                    c = UNITS[v % 4][1]
                    off, w = POFF[c][j], PW[c][j]
                    act.wait_ge(m_ready, sbase + s_index(v, j) + 1)
                    slot = BSLOT[s_(v, j)] if v else SLOT[s_(v, j)]
                    nc.scalar.activation(psb[:, v % 2, off:off + w],
                                         sps[:, slot, :, :].rearrange("p b n -> p (b n)")[:, 0:w], ACT.Exp,
                                         bias=nmax[:, v % 2, j:j + 1], scale=1.0,
                                         accum_out=lsum[:, v % 2, j:j + 1]).then_inc(e_done, 1)

                sb0 = b * S_BATCH
                for q in range(4):
                    q_high_job(q, b * Q_BATCH)
                for j in range(4):
                    exp_job(0, j, sb0)
                act.wait_ge(x_stored, b * 16 + 1)
                with act.Fori(0, PAIRS) as r:
                    sbase = act.snap(b * S_BATCH + r * 16)
                    qbase = act.snap(b * Q_BATCH + r * 4)
                    tbase = act.snap(b * (PAIRS * T_PAIR) + r * T_PAIR)
                    obase = act.snap(b * (PAIRS * 2) + r * 2)
                    def high_job(n):
                        s = t_cols(n)
                        act.wait_ge(t_ready, tbase + n + 1)
                        act.wait_ge(pv_done, tbase + n + 1)
                        nc.scalar.copy(pTh[:, n % 3, s:QC], tps[:, n % 3, s:QC]).then_inc(t_high, 1)

                    def l_job(c):
                        act.wait_ge(l_ps, obase + c + 2)
                        slot = BSLOT[("l", c, 0)]
                        nc.scalar.copy(linv_b[:, c, :], sps[:, slot, 0, :]).then_inc(l_sb, 1)

                    late = []
                    for g in range(4):
                        due = []
                        for what, x in PLAN[g]:
                            for d in due:
                                d[1] -= 1
                            if due and due[0][1] < 0:
                                q_high_job(due.pop(0)[0], qbase)
                            if what == "x" and x[0] == "q":
                                due.append([x[1], 2])
                            if what == "t":
                                high_job(x)
                            elif x[0] == "l":
                                l_job(x[1])
                            if late and (what == "t" or x[0] == "s"):
                                exp_job(*late.pop(), sbase)
                            if what == "x" and x[0] == "s":
                                late.append(x[1:])
                        for d in due:
                            q_high_job(d[0], qbase)
                    for x in late:
                        exp_job(*x, sbase)
                act.wait_ge(q_split, b * Q_BATCH + Q_BATCH)
                for pr in range(PAIRS):
                    if pr >= 2:
                        act.wait_ge(y_used, b * (PAIRS - 1) + pr - 1)
                    nc.scalar.copy(qh[:, pr % 2, :], osb[:, pr, :]).then_inc(oh_rdy, 1)
                    if more and pr == 5:
                        root(b + 1)

            root(0)
            with act.Fori(0, B - 1) as b:
                batch(b, True)
            batch(B - 1, False)

        @block.vector
        def _(dve):
            nc.vector.memset(spot_v.tensor[:], 0.0).then_inc(x_stored, 1)
            nc.vector.memset(nmax[:], 0.0).then_inc(t_low, 3)
            nc.vector.memset(lsum[:], 0.0).then_inc(pv_done, 3)
            nc.vector.memset(linv[:], 0.0).then_inc(o_sb, 1)
            nc.vector.memset(linv_b[:], 0.0).then_inc(l_ps, 1)
            nc.vector.memset(rstd[:], 0.0).then_inc(x2_ready, NT)

            def norm(b, part):
                if part < 4:
                    if part == 0:
                        dve.wait_ge(x_loaded, b * 16 + 16)
                    for i in (2 * part, 2 * part + 1):
                        nc.vector.bn_stats(stats[:, i, :], xb[:, i, :]).then_inc(st1, 1)
                elif part == 4:
                    vector_waits(nc, spot_v, st1, b * NT + NT)
                    for i in range(NT):
                        nc.vector.bn_aggr(aggr[:, i, :], stats[:, i, :]).then_inc(st2, 1)
                    dve.wait_ge(st2, b * NT + NT)
                    nc.vector.tensor_scalar(vareps[:], aggr[:, :, 1], EPS, None, ALU.add).then_inc(st3, 1)
                elif part >= 6:
                    if part == 6:
                        dve.wait_ge(st4, b + 1)
                        nc.vector.reciprocal(rstd[:], std[:]).then_inc(st5, 1)
                        dve.wait_ge(st5, b + 1)
                    for i in range(4 * (part - 6), 4 * (part - 5)):
                        nc.vector.tensor_scalar(xn[:, i, :], xb[:, i, :], aggr[:, i, 0:1], rstd[:, i:i + 1],
                                                ALU.subtract, ALU.mult).then_inc(xn_ready, 1)

            def batch(b, more):
                for n in range(4):
                    k, g = n // 2, n % 2
                    dve.wait_ge(xT_h, b * 4 + n + 1)
                    cols = slice(g * QC, (g + 1) * QC)
                    nc.vector.tensor_tensor(ql[:, k, cols], banks[:, n, :], qh[:, k, cols].bitcast(F32),
                                            ALU.subtract).then_inc(xT_l, 1)
                for c in range(NC2):
                    cols = slice(c * QC, (c + 1) * QC)
                    dve.wait_ge(xq_h, b * 2 + c + 1)
                    nc.vector.tensor_tensor(xq[64:128, cols], banks[64:128, 4 + c, :], xq[64:128, cols].bitcast(F32),
                                            ALU.subtract).then_inc(xq_rdy, 1)
                for c in range(NC2):
                    cols = slice(c * QC, (c + 1) * QC)
                    kb = (6, 0)[c]
                    dve.wait_ge(k_ps, b * 2 + c + 1)
                    nc.vector.tensor_tensor(rot1[:, c, :], banks[:, kb, :], t.cosT[:, cols], ALU.mult)
                    nc.vector.tensor_tensor(rot2[:, c, :], banks[0:64, kb + 1, :], t.sinT[:, cols],
                                            ALU.mult).then_inc(k_rot, 1)
                for g in range(2):
                    dve.wait_ge(v_h, b * 2 + g + 1)
                    nc.vector.tensor_tensor(vl[:, 4 * g:4 * g + 4, 64:128],
                                            banks[:, 2 + g, 0:256].rearrange("p (t c) -> p t c", t=4),
                                            vh[:, 4 * g:4 * g + 4, 64:128].bitcast(F32), ALU.subtract).then_inc(v_rdy, 1)

                def max_job(v, j, sbase):
                    c = UNITS[v % 4][1]
                    dve.wait_ge(s_ready, sbase + s_index(v, j) + 1)
                    slot = BSLOT[s_(v, j)] if v else SLOT[s_(v, j)]
                    nc.vector.tensor_reduce(out=nmax[:, v % 2, j:j + 1],
                                            in_=sps[:, slot, :, :].rearrange("p b n -> p (b n)")[:, 0:PW[c][j]],
                                            axis=AX.X, op=ALU.max, negate=True).then_inc(m_ready, 1)

                def inv_job(v, sbase, rep=None):
                    dve.wait_ge(e_done, sbase + s_index(v, 3) + 1)
                    if rep is not None:
                        dve.wait_ge(l_rep, rep)
                    nc.vector.reciprocal(linv[:, v % 2, :], lsum[:, v % 2, :]).then_inc(l_inv, 1)

                def rot_job(slot, q, qbase):
                    c = UNITS[q % 4][1]
                    cols = slice(c * QC, (c + 1) * QC)
                    dve.wait_ge(q_ps, qbase + q + 1)
                    if q >= 2:
                        dve.wait_ge(q_split, qbase + q - 1)
                    nc.vector.tensor_tensor(rot1[:, q % 2, :], sps[:, slot, 0, :], t.cosT[:, cols], ALU.mult)
                    nc.vector.tensor_tensor(rot2[:, q % 2, :], sps[0:64, slot, 1, :], t.sinT[:, cols],
                                            ALU.mult).then_inc(q_rot, 1)

                dve.wait_ge(k_rdy, b * 2 + 2)
                sb0, qb0 = b * S_BATCH, b * Q_BATCH
                for x in PROLOGUE:
                    if x[0] == "q":
                        rot_job(SLOT[x], x[1], qb0)
                    else:
                        max_job(x[1], x[2], sb0)
                inv_job(0, sb0)
                with dve.Fori(0, PAIRS) as r:
                    sbase = dve.snap(b * S_BATCH + r * 16)
                    qbase = dve.snap(b * Q_BATCH + r * 4)
                    tbase = dve.snap(b * (PAIRS * T_PAIR) + r * T_PAIR)
                    obase = dve.snap(b * (PAIRS * 2) + r * 2)
                    rbase = dve.snap(b * (PAIRS * 4) + r * 4)

                    def low_job(n):
                        s = t_cols(n)
                        dve.wait_ge(t_high, tbase + n + 1)
                        nc.vector.tensor_tensor(pTl[:, n % 3, s:QC], tps[:, n % 3, s:QC],
                                                pTh[:, n % 3, s:QC].bitcast(F32), ALU.subtract).then_inc(t_low, 1)

                    def o_job(c):
                        dve.wait_ge(pv_done, tbase + sum(TU[:2 * c + 2]) + 3)
                        dve.wait_ge(l_sb, obase + c + 1)
                        nc.vector.tensor_tensor(osb[:, bass.ds(r, 1), c * QC:(c + 1) * QC]
                                                .rearrange("p a n -> p (a n)"),
                                                ops, linv_b[:, c, :], ALU.mult).then_inc(o_sb, 1)

                    for g in range(4):
                        seen = 0
                        for what, x in PLAN[g]:
                            if what == "t":
                                low_job(x)
                                if x == sum(TU[:2]) + 1:
                                    o_job(0)
                                seen += 1
                                if seen == 1 and g > 0:
                                    inv_job(g, sbase, rbase + g)
                            elif x[0] == "q":
                                rot_job(BSLOT[x], x[1], qbase)
                            elif x[0] == "s":
                                max_job(x[1], x[2], sbase)
                    inv_job(4, sbase, rbase + 4)
                    o_job(1)
                for pr in range(PAIRS):
                    dve.wait_ge(oh_rdy, b * PAIRS + pr + 1)
                    nc.vector.tensor_tensor(ql[:, pr % 2, :], osb[:, pr, :], qh[:, pr % 2, :].bitcast(F32),
                                            ALU.subtract).then_inc(ol_rdy, 1)
                    if more:
                        norm(b + 1, pr)
                dve.wait_ge(x_again, b * 16 + 16)
                for i in range(NT):
                    dve.wait_ge(y_ready, b * NT + i + 1)
                    nc.vector.tensor_tensor(x2b[:, i, :], banks[:, i, 0:D], x2b[:, i, :], ALU.add).then_inc(x2_ready, 1)

            for part in range(8):
                norm(0, part)
            nc.vector.memset(vh[:].bitcast(F32), 0.0).then_inc(zeroed, 1)
            nc.vector.memset(vl[:].bitcast(F32), 0.0).then_inc(zeroed, 1)
            with dve.Fori(0, B - 1) as b:
                batch(b, True)
            batch(B - 1, False)

        @block.gpsimd
        def _(pool):
            def split(buf, oh, ol, added, high, done, n):
                nc.gpsimd.tensor_tensor(rot1[0:64, buf, :], rot1[0:64, buf, :], rot2[:, buf, :], ALU.add)\
                    .then_inc(added, 1)
                pool.wait_ge(high, n + 1)
                nc.gpsimd.tensor_tensor(ol, rot1[:, buf, :], oh.bitcast(F32), ALU.subtract).then_inc(done, 1)

            nc.gpsimd.memset(ones[:], 1.0).then_inc(l_rep, 1)
            pool.wait_ge(l_rep, 1)
            with pool.Fori(0, B) as b:
                for c in range(NC2):
                    pool.wait_ge(k_rot, b * 2 + c + 1)
                    cols = slice(c * QC, (c + 1) * QC)
                    split(c, kTh[:, cols], kTl[:, cols], k_add, k_high, k_rdy, b * 2 + c)

                def split_job(q, qbase):
                    a, c = UNITS[q % 4]
                    cols = slice(c * QC, (c + 1) * QC)
                    pool.wait_ge(q_rot, qbase + q + 1)
                    split(q % 2, qh[:, a, cols], ql[:, a, cols], q_add, q_high, q_split, qbase + q)

                for q in range(4):
                    split_job(q, b * Q_BATCH)
                with pool.Fori(0, PAIRS) as r:
                    qbase = pool.snap(b * Q_BATCH + r * 4)
                    ubase = pool.snap(b * (PAIRS * 4 + 1) + r * 4)

                    def rep_job(u):
                        a, c = UNITS[u]
                        pool.wait_ge(l_inv, ubase + u + 1)
                        if a == 0:
                            pool.wait_ge(l_ps, rbase_o + c)
                        nc.gpsimd.tensor_tensor(lrep[:, :, 64 * a:64 * a + 64],
                                                linv[:, u % 2, :].unsqueeze(2).to_broadcast([P, 4, 64]),
                                                ones[:].unsqueeze(2).to_broadcast([P, 4, 64]), ALU.mult)\
                            .then_inc(l_rep, 1)

                    rbase_o = pool.snap(b * (PAIRS * 2) + r * 2 + 1)
                    rep_job(0)
                    rep_job(1)
                    rep_job(2)
                    for q in range(4, 7):
                        split_job(q, qbase)
                    rep_job(3)
                    split_job(7, qbase)


def ffn(nc, t, ins, out):
    NG = B
    HT, HN = NT // 2, N // 2
    with ExitStack() as ctx:
        def sb(name, shape, dt=F32):
            return ctx.enter_context(nc.sbuf_tensor(name, shape, dt))

        def sem(name):
            return ctx.enter_context(nc.semaphore(name))

        raw = sb("f_raw", [P, 3, MC * D])
        wth, wtl = sb("wth", [P, KC, 2 * GI], F32R), sb("wtl", [P, KC, 2 * GI], F32R)
        dh, dl = sb("dh", [P, MC, D], F32R), sb("dl", [P, MC, D], F32R)
        mu_raw, mu4 = sb("mu_raw", [P, KC, G, GS]), sb("mu4", [P, KC, G, 32])
        mwh, mwl = sb("mwh", [P, GU], F32R), sb("mwl", [P, GU])
        mw = sb("mw", [P, G, GU], F32R)
        gw_raw = sb("gw_raw", [E, D])
        gwh, gwl = sb("gwh", [P, KC, E], F32R), sb("gwl", [P, KC, E], F32R)
        hl_mask, eid = sb("hl_mask", [P, 2]), sb("eid", [P, 2])
        words = ins["inv_map"].shape[0] // E
        inv_raw = sb("inv_raw", [P, words * E], I32)
        inv_f, inv_n, onehot = sb("inv_f", [P, E]), sb("inv_n", [P, E]), sb("onehot", [P, 2, E])

        x2 = sb("x2", [P, NT, D])
        spot_v = Spots(sb("f_spot_v", [1, 64]))
        xn = raw[:, 0, 0:HT * D].rearrange("p (t d) -> p t d", t=HT)
        xTh, xTl = sb("f_xTh", [P, KC, N], F32R), sb("f_xTl", [P, KC, N], F32R)
        stats, aggr = sb("f_stats", [P, HT, 6]), sb("f_aggr", [P, HT, 2])
        vareps, std, rstd = sb("f_vareps", [P, HT]), sb("f_std", [P, HT]), sb("f_rstd", [P, HT])
        r1, r8 = sb("r1", [P, HT]), sb("r8", [P, HT * G])
        lg, sc, rest, wsel = (raw[:, 1, n * HT * E:(n + 1) * HT * E].rearrange("p (t e) -> p t e", t=HT)
                              for n in range(4))
        top = sb("top", [P, HT, 8])
        wselT = sb("wselT", [P, 2, P])
        soft_h = sb("soft_h", [P, HT * G, GS], F32R)
        sst = raw[:, 2, 0:HT * G * 32].rearrange("p (m s) -> p m s", s=32)
        sT = sb("sT", [P, 2, N], F32R)
        mass = sb("mass", [P, NT, G])
        sg = sb("sg", [P, 4, I])
        act_sb = sb("act_sb", [P, 2, GI])
        aTh, aTl = sb("aTh", [P, 2, MC, P], F32R), sb("aTl", [P, 2, MC, P], F32R)

        banks = ctx.enter_context(nc.psum_tensor("fps", [P, 8, 512], F32))

        w_loaded = [sem(n) for n in ("gate_loaded", "up_loaded", "down_loaded")]
        mu_loaded, r_loaded, chain = sem("mask_up_loaded"), sem("router_loaded"), sem("f_dve_chain")
        w_ps, w_h, w_l = sem("f_w_ps"), sem("f_w_high"), sem("f_w_low")
        mu_rdy, mw_ps, mw_h, mw_rdy = sem("mu_ready"), sem("mw_ps"), sem("mw_high"), sem("mw_ready")
        x_loaded = [sem(f"f_x_loaded_{h}") for h in range(2)]
        x_stored = sem("f_x_stored")
        st1, st2, st3, st4 = sem("f_stats_done"), sem("f_aggr_done"), sem("f_vareps_done"), sem("f_std_done")
        xn_ready, xT_ps, xT_h, xT_l = sem("f_xn_ready"), sem("f_xT_ps"), sem("f_xT_h"), sem("f_xT_l")
        lg_ps, lg_sub, lg_exp, w_sel = sem("logits_ps"), sem("logits_shifted"), sem("logits_exp"), sem("w_selected")
        wT_ps, wT_sb, fl_ps, fl_sub, fl_exp = (sem("wselT_ps"), sem("wselT_sb"), sem("flat_ps"), sem("flat_shifted"),
                                               sem("flat_exp"))
        soft_rdy, sT_ps, sT_rdy = sem("soft_ready"), sem("sT_ps"), sem("sT_ready")
        gu_ps, silu_done, a_ready = sem("gate_up_ps"), sem("silu_done"), sem("a_ready")
        aT_ps, aT_h, aT_l, y_ps, o_ready = sem("aT_ps"), sem("aT_high"), sem("aT_low"), sem("y_ps"), sem("out_ready")

        block = ctx.enter_context(nc.Block())
        x2_v = t.x2_dram.rearrange("b (t p) d -> b p t d", p=P)
        out_v = out.rearrange("b (t p) d -> b p t d", p=P)
        raw_w = raw[:].rearrange("p w (m d) -> p w m d", m=MC)
        raw_d = raw[:, 2, :].rearrange("p (k c) -> p k c", k=KC)

        WJOBS = [("w", w, k, m, min(4, MC - m)) for w in range(2) for k in range(KC) for m in range(0, MC, 4)]
        WJOBS += [("d", 0, 0, m, min(2, MC - m)) for m in range(0, MC, 2)]
        WJOBS += [("r", 0, 0, 0, KC)]

        def w_dest(job, hi):
            kind, w, k, m, n = job
            if kind == "w":
                return (wth if hi else wtl)[:, k, w * GI + m * P:w * GI + (m + n) * P]
            if kind == "d":
                return (dh if hi else dl)[:, m:m + n, :].rearrange("p m d -> p (m d)")
            return (gwh if hi else gwl)[:].rearrange("p k e -> p (k e)")

        def w_bank(j):
            kind, _, _, _, n = WJOBS[j]
            width = n * (P if kind == "w" else D if kind == "d" else E)
            return banks[:, j % 6, 0:width]

        WINDOW = (4, 42)
        PE_AT = {6: 0, 8: 1, 10: 2, 16: 3, 18: 4, 26: 5, 27: 6}
        ACT_AT = {2: 0, 6: 1, 8: 2, 11: 3, 16: 4, 20: 5, 26: 6, 27: 7}
        DVE_AT = {0: 0, 1: 1, 3: 2, 6: 3, 8: 4, 10: 5, 12: 6, 13: 7, 14: 8, 18: 9, 19: 10, 21: 11, 22: 12}

        def due(at, n, h):
            return at.get(n - WINDOW[1 - h])

        assert WINDOW[0] + max(ACT_AT) < HT * G and WINDOW[1] + max(ACT_AT) < (NT + 1) * G

        @block.sync
        def _(sp):
            for w, name in ((0, "gate_proj_w"), (1, "up_proj_w")):
                sp.dma_start(raw_w[:, w], ins[name].rearrange("g i d -> (g i) d").rearrange("(m p) d -> p m d", p=P))\
                    .then_inc(w_loaded[w], 16)
            for g in range(G):
                sp.dma_start(raw_d[:, :, g * I:(g + 1) * I],
                             ins["down_proj_w"][g].rearrange("(k p) i -> p k i", p=P)).then_inc(w_loaded[2], 16)
            for k in range(KC):
                sp.dma_start(mu_raw[:, k], ins["mask_up_w"][:, k * P:(k + 1) * P, :].rearrange("g p i -> p g i"))\
                    .then_inc(mu_loaded, 16)
            sp.dma_start(gw_raw[:], ins["gate_w"]).then_inc(r_loaded, 16)
            sp.dma_start(hl_mask[:], ins["hl_mask"]).then_inc(r_loaded, 16)
            sp.dma_start(eid[:], ins["eid"]).then_inc(r_loaded, 16)
            sp.dma_start(inv_raw[:], ins["inv_map"].partition_broadcast(P)).then_inc(r_loaded, 16)

            def load(b, h):
                sp.dma_start(x2[:, HT * h:HT * (h + 1), :],
                             x2_v[bass.ds(b, 1), :, HT * h:HT * (h + 1), :].rearrange("a p t d -> (a p) t d"))\
                    .then_inc(x_loaded[h], 16)

            def store(b, h):
                sp.wait_ge(o_ready, b * NT + HT * (h + 1))
                sp.dma_start(out_v[bass.ds(b, 1), :, HT * h:HT * (h + 1), :].rearrange("a p t d -> (a p) t d"),
                             x2[:, HT * h:HT * (h + 1), :]).then_inc(x_stored, 16)

            load(0, 0)
            load(0, 1)
            with sp.Fori(0, NG - 1) as b:
                for h in range(2):
                    store(b, h)
                    sp.wait_ge(x_stored, b * 32 + 16 * (h + 1))
                    load(b + 1, h)
            for h in range(2):
                store(NG - 1, h)
            sp.wait_ge(x_stored, 32 * NG)

        @block.tensor
        def _(pe):
            for j, (kind, w, k, m, n) in enumerate(WJOBS):
                if kind == "w" and k == 0 and m == 0:
                    pe.wait_ge(w_loaded[w], 16)
                elif kind == "d" and m == 0:
                    pe.wait_ge(w_loaded[2], 16 * G)
                elif kind == "r":
                    pe.wait_ge(r_loaded, 16 * 4)
                if j >= 6:
                    pe.wait_ge(w_l, j - 5)
                if kind == "w":
                    for i in range(n):
                        last = nc.tensor.transpose(banks[:, j % 6, i * P:(i + 1) * P],
                                                   raw_w[:, w, m + i, k * P:(k + 1) * P], t.ident[:])
                elif kind == "d":
                    for i in range(n):
                        for kk in range(KC):
                            last = nc.tensor.transpose(banks[:, j % 6, i * D + kk * P:i * D + (kk + 1) * P],
                                                       raw_d[:, kk, (m + i) * P:(m + i + 1) * P], t.ident[:])
                else:
                    for kk in range(KC):
                        last = nc.tensor.transpose(banks[:, j % 6, kk * E:(kk + 1) * E],
                                                   gw_raw[:, kk * P:(kk + 1) * P], t.ident[0:E, 0:E])
                last.then_inc(w_ps, 1)
            pe.wait_ge(w_l, len(WJOBS))
            pe.wait_ge(mu_rdy, 4)
            for q in range(2):
                for gg in range(4):
                    g = 4 * q + gg
                    n = 0
                    for k in range(KC):
                        for part in (wth, wtl):
                            rhs = part[:, k, :].bitcast(F32).rearrange("p (w c) -> p w c", w=2)[:, :, g * I:(g + 1) * I]
                            last = mm(nc, banks[32 * gg:32 * gg + 32, 6 + q, 0:GU].rearrange("p (w c) -> p w c", w=2),
                                      mu4[:, k, g, :], rhs, n == 0, n == 3)
                            n += 1
                last.then_inc(mw_ps, 1)

            pe.wait_ge(mw_rdy, 2)

            def router(b, h, part):
                H = 2 * b + h
                bank = banks[:, 3, :]
                if part in (0, 1):
                    k = part
                    if k == 0:
                        pe.wait_ge(xn_ready, H * HT + HT)
                    else:
                        pe.wait_ge(xT_l, H * 2 + 1)
                    for i in range(HT):
                        last = nc.tensor.transpose(bank[:, i * P:(i + 1) * P], xn[:, i, k * P:(k + 1) * P], t.ident[:])
                    last.then_inc(xT_ps, 1)
                elif part == 2:
                    pe.wait_ge(xT_l, H * 2 + 2)
                    for i in range(HT):
                        tok = slice(h * HN + i * P, h * HN + (i + 1) * P)
                        for k in range(KC):
                            for n, (x, w) in enumerate(((xTh, gwh), (xTh, gwl), (xTl, gwh))):
                                last = mm(nc, bank[:, i * E:(i + 1) * E], x[:, k, tok], w[:, k, :],
                                          k == 0 and n == 0, k == KC - 1 and n == 2)
                    last.then_inc(lg_ps, 1)
                elif part == 3:
                    pe.wait_ge(w_sel, H + 1)
                    for i in range(HT // 2):
                        last = nc.tensor.transpose(bank[:, i * P:(i + 1) * P],
                                                   wsel[:, 2 * i:2 * i + 2, :].rearrange("p t e -> p (t e)"), t.ident[:])
                    last.then_inc(wT_ps, 1)
                elif part == 4:
                    pe.wait_ge(wT_sb, H + 1)
                    for i in range(HT):
                        last = mm(nc, bank[:, i * E:(i + 1) * E], wselT[:, i // 2, :], onehot[:, i % 2, :], True, True)
                    last.then_inc(fl_ps, 1)
                elif part in (5, 6):
                    q = part - 5
                    if q == 0:
                        pe.wait_ge(soft_rdy, H * 4 + 4)
                    else:
                        pe.wait_ge(sT_rdy, H * 2 + 1)
                    for i in range(HT):
                        src = sst[:, i * G + 4 * q:i * G + 4 * q + 4, :].rearrange("p g s -> p (g s)")
                        last = nc.tensor.transpose(bank[:, i * P:(i + 1) * P], src, t.ident[:])
                    last.then_inc(sT_ps, 1)

            def group(b, more):
                def gate_up(i, g):
                    n = i * G + g
                    if i % HT == 0 and g == 0:
                        pe.wait_ge(sT_rdy, b * 4 + 2 * (i // HT) + 2)
                    if n >= 3:
                        pe.wait_ge(a_ready, b * (NT * G) + n - 2)
                    tok = slice(i * P, (i + 1) * P)
                    ps = banks[:, n % 3, 0:GU]
                    ps2 = ps.rearrange("p (w c) -> p w c", w=2)

                    def cols(w, k):
                        return w[:, k, :].rearrange("p (w c) -> p w c", w=2)[:, :, g * I:(g + 1) * I]
                    mm(nc, ps, sT[:, g // 4, tok], mw[:, g, :], True, False)
                    for k in range(KC):
                        for j, (x, w) in enumerate(((xTh, wth), (xTh, wtl), (xTl, wth))):
                            last = mm(nc, ps2, x[:, k, tok], cols(w, k), False, k == KC - 1 and j == 2)
                    last.then_inc(gu_ps, 1)

                def transposes(i):
                    pe.wait_ge(a_ready, b * (NT * G) + (i + 1) * G)
                    for q in range(3):
                        if i >= 1:
                            pe.wait_ge(aT_l, b * (NT * 3) + 3 * i + q - 2)
                        for m in range(4 * q, min(4 * q + 4, MC)):
                            last = nc.tensor.transpose(banks[:, 4 + q, (m - 4 * q) * P:(m - 4 * q + 1) * P],
                                                       act_sb[:, i % 2, m * P:(m + 1) * P], t.ident[:])
                        last.then_inc(aT_ps, 1)

                def down(i):
                    if i >= 1:
                        pe.wait_ge(o_ready, b * NT + i)
                    pe.wait_ge(aT_l, b * (NT * 3) + 3 * i + 3)
                    for m in range(MC):
                        for j, (a, w) in enumerate(((aTh, dh), (aTh, dl), (aTl, dh))):
                            last = mm(nc, banks[:, 7, 0:D], a[:, i % 2, m, :], w[:, m, :],
                                      m == 0 and j == 0, m == MC - 1 and j == 2)
                    last.then_inc(y_ps, 1)

                for i in range(NT + 1):
                    for g in range(G):
                        if i < NT:
                            gate_up(i, g)
                        if i >= 1 and g == 2:
                            transposes(i - 1)
                        if i >= 1 and g == 5:
                            down(i - 1)
                        for h in range(0 if more else 1, 2):
                            router(b + 1 - h, h, due(PE_AT, i * G + g, h))

            for part in range(7):
                router(0, 0, part)
            with pe.Fori(0, NG - 1) as b:
                group(b, True)
            group(NG - 1, False)

        @block.scalar
        def _(act):
            for j, job in enumerate(WJOBS):
                act.wait_ge(w_ps, j + 1)
                nc.scalar.copy(w_dest(job, True), w_bank(j)).then_inc(w_h, 1)
            for q in range(2):
                act.wait_ge(mw_ps, q + 1)
                if q >= 1:
                    act.wait_ge(mw_rdy, q)
                nc.scalar.copy(mwh[:], banks[:, 6 + q, 0:GU]).then_inc(mw_h, 1)

            def router(b, h, part):
                H = 2 * b + h
                bank = banks[:, 3, :]
                cols = slice(h * HN, (h + 1) * HN)
                if part == 0:
                    act.wait_ge(st3, H + 1)
                    nc.scalar.activation(std[:], vareps[:], ACT.Sqrt).then_inc(st4, 1)
                elif part in (1, 2):
                    act.wait_ge(xT_ps, H * 2 + part)
                    nc.scalar.copy(xTh[:, part - 1, cols], bank).then_inc(xT_h, 1)
                elif part == 3:
                    act.wait_ge(lg_sub, H + 1)
                    nc.scalar.activation(sc, lg, ACT.Exp).then_inc(lg_exp, 1)
                elif part == 4:
                    act.wait_ge(wT_ps, H + 1)
                    nc.scalar.copy(wselT[:].rearrange("p a n -> p (a n)"), bank[:, 0:HT // 2 * P]).then_inc(wT_sb, 1)
                elif part == 5:
                    act.wait_ge(fl_sub, H + 1)
                    nc.scalar.activation(sc, lg, ACT.Exp).then_inc(fl_exp, 1)
                elif part in (6, 7):
                    act.wait_ge(sT_ps, H * 2 + part - 5)
                    nc.scalar.copy(sT[:, part - 6, cols], bank).then_inc(sT_rdy, 1)

            def group(b, more):
                def high(i):
                    for q in range(3):
                        act.wait_ge(aT_ps, b * (NT * 3) + 3 * i + q + 1)
                        if i >= 2 and q == 0:
                            act.wait_ge(y_ps, b * NT + i - 1)
                        n = min(4, MC - 4 * q)
                        nc.scalar.copy(aTh[:, i % 2, 4 * q:4 * q + n, :].rearrange("p m n -> p (m n)"),
                                       banks[:, 4 + q, 0:n * P]).then_inc(aT_h, 1)

                for i in range(NT + 1):
                    for g in range(G):
                        if i < NT:
                            n = i * G + g
                            act.wait_ge(gu_ps, b * (NT * G) + n + 1)
                            nc.scalar.activation(sg[:, g % 4, :], banks[:, n % 3, 0:I], ACT.Silu)\
                                .then_inc(silu_done, 1)
                        if i >= 1 and g == 2:
                            high(i - 1)
                        for h in range(0 if more else 1, 2):
                            router(b + 1 - h, h, due(ACT_AT, i * G + g, h))

            for part in range(8):
                router(0, 0, part)
            with act.Fori(0, NG - 1) as b:
                group(b, True)
            group(NG - 1, False)

        @block.vector
        def _(dve):
            nc.vector.memset(spot_v.tensor[:], 0.0)
            nc.vector.memset(mw[:].bitcast(F32), 0.0)
            for j, job in enumerate(WJOBS):
                dve.wait_ge(w_h, j + 1)
                nc.vector.tensor_tensor(w_dest(job, False), w_bank(j), w_dest(job, True).bitcast(F32),
                                        ALU.subtract).then_inc(w_l, 1)
            dve.wait_ge(mu_loaded, 16 * KC)
            for c in range(4):
                nc.vector.tensor_copy(mu4[:, :, :, c * GS:(c + 1) * GS], mu_raw[:]).then_inc(mu_rdy, 1)
            dve.wait_ge(r_loaded, 16 * 4)
            nc.vector.tensor_copy(inv_f[:], inv_raw[:].rearrange("p (e w) -> p e w", w=words)[:, :, 0]).then_inc(chain, 1)
            dve.wait_ge(chain, 1)
            nc.vector.tensor_scalar(inv_n[:], inv_f[:], 0.0, float(E), ALU.is_lt, ALU.mult).then_inc(chain, 1)
            dve.wait_ge(chain, 2)
            nc.vector.tensor_tensor(inv_f[:], inv_f[:], inv_n[:], ALU.add).then_inc(chain, 1)
            dve.wait_ge(chain, 3)
            for h in range(2):
                nc.vector.tensor_scalar(onehot[:, h, :], inv_f[:], eid[:, h:h + 1], None, ALU.is_equal)
            for q in range(2):
                dve.wait_ge(mw_h, q + 1)
                nc.vector.tensor_tensor(mwl[:], banks[:, 6 + q, 0:GU], mwh[:].bitcast(F32), ALU.subtract).then_inc(chain, 1)
                dve.wait_ge(chain, 4 + 2 * q)
                nc.vector.tensor_scalar(mwl[:], mwl[:], hl_mask[:, 1:2], None, ALU.mult).then_inc(chain, 1)
                dve.wait_ge(chain, 5 + 2 * q)
                for gg in range(4):
                    rows = slice(32 * gg, 32 * gg + 32)
                    last = nc.vector.scalar_tensor_tensor(out=mw[rows, 4 * q + gg, :], in0=mwh[rows, :].bitcast(F32),
                                                          scalar=hl_mask[rows, 0:1], in1=mwl[rows, :],
                                                          op0=ALU.mult, op1=ALU.add)
                last.then_inc(mw_rdy, 1)
            CH0, CHB = 7, 13


            def router(b, h, part):
                H = 2 * b + h
                bank = banks[:, 3, :]
                tiles = slice(HT * h, HT * (h + 1))
                done = {2: 0, 5: 1, 6: 2, 7: 5, 8: 6, 9: 7, 10: 8, 11: 10}
                count = [done.get(part, 0)]

                def step(ins_, wait=dve.wait_ge):
                    count[0] += 1
                    ins_.then_inc(chain, 1)
                    wait(chain, H * CHB + CH0 + count[0])

                def apart(semaphore, value):
                    vector_waits(nc, spot_v, semaphore, value)

                if part == 0:
                    dve.wait_ge(x_loaded[h], b * 16 + 16)
                    for i in range(HT):
                        nc.vector.bn_stats(stats[:, i, :], x2[:, HT * h + i, :]).then_inc(st1, 1)
                elif part == 1:
                    vector_waits(nc, spot_v, st1, H * HT + HT)
                    for i in range(HT):
                        nc.vector.bn_aggr(aggr[:, i, :], stats[:, i, :]).then_inc(st2, 1)
                    dve.wait_ge(st2, H * HT + HT)
                    nc.vector.tensor_scalar(vareps[:], aggr[:, :, 1], EPS, None, ALU.add).then_inc(st3, 1)
                elif part == 2:
                    dve.wait_ge(st4, H + 1)
                    step(nc.vector.reciprocal(rstd[:], std[:]))
                    for i in range(HT):
                        nc.vector.tensor_scalar(xn[:, i, :], x2[:, HT * h + i, :], aggr[:, i, 0:1], rstd[:, i:i + 1],
                                                ALU.subtract, ALU.mult).then_inc(xn_ready, 1)
                elif part in (3, 4):
                    k, cols = part - 3, slice(h * HN, (h + 1) * HN)
                    dve.wait_ge(xT_h, H * 2 + k + 1)
                    nc.vector.tensor_tensor(xTl[:, k, cols], bank, xTh[:, k, cols].bitcast(F32),
                                            ALU.subtract).then_inc(xT_l, 1)
                elif part == 5:
                    dve.wait_ge(lg_ps, H + 1)
                    lg_v = bank[:, 0:HT * E].rearrange("p (t e) -> p t e", t=HT)
                    step(nc.vector.tensor_reduce(out=r1[:], in_=lg_v, axis=AX.X, op=ALU.max))
                    nc.vector.tensor_tensor(lg, lg_v, r1[:].unsqueeze(2).to_broadcast([P, HT, E]), ALU.subtract)\
                        .then_inc(lg_sub, 1)
                elif part == 6:
                    dve.wait_ge(lg_exp, H + 1)
                    step(nc.vector.tensor_reduce(out=r1[:], in_=sc, axis=AX.X, op=ALU.add))
                    step(nc.vector.reciprocal(r1[:], r1[:]))
                    step(nc.vector.tensor_tensor(sc, sc, r1[:].unsqueeze(2).to_broadcast([P, HT, E]), ALU.mult), apart)
                elif part == 7:
                    for i in range(HT):
                        last = nc.vector.max(out=top[:, i, :], in_=sc[:, i, :])
                    step(last, apart)
                elif part == 8:
                    for i in range(HT):
                        last = nc.vector.match_replace(out=rest[:, i, :], in_to_replace=top[:, i, :],
                                                       in_values=sc[:, i, :], imm_value=0.0)
                    step(last)
                    nc.vector.tensor_tensor(wsel, sc, rest, ALU.subtract).then_inc(w_sel, 1)
                elif part in (9, 10, 11):
                    fl = bank[:, 0:HT * E].rearrange("p (m s) -> p m s", s=GS)
                    lgf = lg.rearrange("p t (g s) -> p (t g) s", s=GS)
                    scf = sc.rearrange("p t (g s) -> p (t g) s", s=GS)
                    if part == 9:
                        dve.wait_ge(fl_ps, H + 1)
                        nc.vector.tensor_reduce(out=mass[:, tiles, :].rearrange("p t g -> p (t g)"), in_=fl,
                                                axis=AX.X, op=ALU.add)
                        step(nc.vector.tensor_scalar(lgf, fl, 0.0, -1.0e9, ALU.is_equal, ALU.mult))
                    elif part == 10:
                        step(nc.vector.tensor_tensor(lgf, fl, lgf, ALU.add))
                        step(nc.vector.tensor_reduce(out=r8[:], in_=lgf, axis=AX.X, op=ALU.max))
                        nc.vector.tensor_tensor(lgf, lgf, r8[:].unsqueeze(2).to_broadcast([P, HT * G, GS]),
                                                ALU.subtract).then_inc(fl_sub, 1)
                    else:
                        dve.wait_ge(fl_exp, H + 1)
                        step(nc.vector.tensor_reduce(out=r8[:], in_=scf, axis=AX.X, op=ALU.add))
                        step(nc.vector.reciprocal(r8[:], r8[:]))
                        step(nc.vector.tensor_tensor(scf, scf, r8[:].unsqueeze(2).to_broadcast([P, HT * G, GS]),
                                                     ALU.mult))
                        assert count[0] == CHB, count
                elif part == 12:
                    scf = sc.rearrange("p t (g s) -> p (t g) s", s=GS)
                    nc.vector.tensor_copy(soft_h[:], scf).then_inc(soft_rdy, 1)
                    dve.wait_ge(soft_rdy, H * 4 + 1)
                    nc.vector.tensor_copy(sst.rearrange("p m (r h s) -> p m r h s", r=2, h=2)[:, :, :, 0, :],
                                          soft_h[:].bitcast(F32).unsqueeze(2).to_broadcast([P, HT * G, 2, GS]))\
                        .then_inc(soft_rdy, 1)
                    for r in range(2):
                        nc.vector.tensor_tensor(sst[:, :, (2 * r + 1) * GS:(2 * r + 2) * GS], scf,
                                                soft_h[:].bitcast(F32), ALU.subtract).then_inc(soft_rdy, 1)

            def group(b, more):
                def low(i):
                    for q in range(3):
                        dve.wait_ge(aT_h, b * (NT * 3) + 3 * i + q + 1)
                        n = min(4, MC - 4 * q)
                        nc.vector.tensor_tensor(aTl[:, i % 2, 4 * q:4 * q + n, :].rearrange("p m n -> p (m n)"),
                                                banks[:, 4 + q, 0:n * P],
                                                aTh[:, i % 2, 4 * q:4 * q + n, :].rearrange("p m n -> p (m n)").bitcast(F32),
                                                ALU.subtract).then_inc(aT_l, 1)

                for i in range(NT + 1):
                    for g in range(G):
                        if i < NT:
                            n = i * G + g
                            dve.wait_ge(silu_done, b * (NT * G) + n + 1)
                            nc.vector.scalar_tensor_tensor(out=act_sb[:, i % 2, g * I:(g + 1) * I],
                                                           in0=banks[:, n % 3, I:GU], scalar=mass[:, i, g:g + 1],
                                                           in1=sg[:, g % 4, :], op0=ALU.mult, op1=ALU.mult)\
                                .then_inc(a_ready, 1)
                        if i >= 1 and g == 2:
                            low(i - 1)
                        if i >= 1 and g == 7:
                            dve.wait_ge(y_ps, b * NT + i)
                            nc.vector.tensor_tensor(x2[:, i - 1, :], banks[:, 7, 0:D], x2[:, i - 1, :], ALU.add)\
                                .then_inc(o_ready, 1)
                        for h in range(0 if more else 1, 2):
                            router(b + 1 - h, h, due(DVE_AT, i * G + g, h))

            for part in range(13):
                router(0, 0, part)
            with dve.Fori(0, NG - 1) as b:
                group(b, True)
            group(NG - 1, False)


class Shared:
    pass


def build(nc, ins, out):
    with ExitStack() as ctx:
        t = Shared()
        t.wq_dram = nc.dram_tensor("wq_scratch", [PAIRS + 1, P, 2, 2, 192], F32, kind="Internal").ap()
        t.x2_dram = nc.dram_tensor("x2_scratch", [B, N, D], F32, kind="Internal").ap()
        t.ident = ctx.enter_context(nc.sbuf_tensor("ident", [P, P], F32))
        with ExitStack() as at:
            def sb(name, shape, dt=F32):
                return at.enter_context(nc.sbuf_tensor(name, shape, dt))
            t.ident_b, t.mask_b = sb("ident_b", [P, P], BF16), sb("mask_b", [P, P], BF16)
            t.cosT, t.sinT = sb("cosT", [P, N]), sb("sinT", [64, N])
            t.wk = sb("wk", [P, 2, KC, 192], F32R)
            t.wqa = sb("wqa", [P, 2, KC, P], F32R)
            t.w2h, t.w2l = sb("w2h", [P, PAIRS, D], F32R), sb("w2l", [P, PAIRS, D], F32R)
            t.xb = sb("xb", [P, NT, D])
            t.x_loaded = at.enter_context(nc.semaphore("x_loaded"))
            attention_weights(nc, t, ins)
            attention(nc, t, ins)
        ffn(nc, t, ins, out)


def constants():
    j = np.arange(ROPE // 2)
    theta = (10000.0 ** (-2.0 * j / ROPE)).astype(np.float32)
    ang = (np.arange(N, dtype=np.float32)[:, None] * theta[None, :]).astype(np.float64)
    cos, sin = np.cos(ang).T.astype(np.float32), np.sin(ang).T.astype(np.float32)
    p = np.arange(P)
    return {
        "ident": np.eye(P, dtype=np.float32),
        "mask": np.where(p[None, :] > p[:, None], NEG, 0.0).astype(np.float32),
        "cos": np.ascontiguousarray(np.concatenate([cos, cos, np.ones((64, N), np.float32)])),
        "sin": np.ascontiguousarray(np.concatenate([-sin, sin])),
        "hl_mask": np.stack([(p % 32 < 16), (p % 32 >= 16)], 1).astype(np.float32),
        "eid": np.stack([np.where(p // 64 == h, p % 64, -1) for h in range(2)], 1).astype(np.float32),
    }


def kernel(L0_attn_x, L0_attn_Wqa, L0_attn_Wqb, L0_attn_Wkva, L0_attn_Wkvb, L0_attn_Wout, L0_ffn_gate_w,
           L0_ffn_mask_up_w, L0_ffn_gate_proj_w, L0_ffn_up_proj_w, L0_ffn_down_proj_w, L0_ffn_inv_map):
    import concourse.bacc as bacc
    from concourse.bass_utils import run_bass_kernel_spmd

    nc = bacc.Bacc("TRN2", target_bir_lowering=False, num_devices=1)
    arrays = {"x": L0_attn_x, "Wqa": L0_attn_Wqa, "Wqb": L0_attn_Wqb, "Wkva": L0_attn_Wkva, "Wkvb": L0_attn_Wkvb,
              "Wout": L0_attn_Wout, "gate_w": L0_ffn_gate_w, "mask_up_w": L0_ffn_mask_up_w,
              "gate_proj_w": L0_ffn_gate_proj_w, "up_proj_w": L0_ffn_up_proj_w, "down_proj_w": L0_ffn_down_proj_w}
    arrays = {k: np.ascontiguousarray(v) for k, v in arrays.items()}
    arrays["inv_map"] = np.ascontiguousarray(L0_ffn_inv_map).reshape(-1).view(np.int32)
    arrays.update(constants())
    ins, feed = {}, {}
    for k, v in arrays.items():
        ins[k] = nc.dram_tensor(f"in_{k}", v.shape, mybir.dt.from_np(v.dtype), kind="ExternalInput").ap()
        feed[f"in_{k}"] = v
    out = nc.dram_tensor("out", (B, N, D), F32, kind="ExternalOutput").ap()
    build(nc, ins, out)
    r = run_bass_kernel_spmd(nc, [feed], core_ids=[0])
    return r.results[0]["out"]
```
